# Optimizing a Trainium2 kernel written in Bass

```python
import numpy as np
import jax
import jax.numpy as jnp

def _softmax(x, axis=-1):
    return jax.nn.softmax(x, axis=axis)

def _gelu(x):
    return jax.nn.gelu(x, approximate=True)

def _silu(x):
    return jax.nn.silu(x)

def _sigmoid(x):
    return jax.nn.sigmoid(x)

def _layernorm(x, axis=-1, eps=1e-05):
    m = jnp.mean(x, axis=axis, keepdims=True)
    v = jnp.var(x, axis=axis, keepdims=True)
    return (x - m) / jnp.sqrt(v + eps)

def _scatter_add(tgt, idx, src, axis=0):
    return tgt.at[idx].add(src)

def _segment_sum(src, seg, n):
    return jax.ops.segment_sum(src, seg, n)
kernel_name = 'mk_gnn_preln_d1_gnn_r8_3109e3'

def setup_inputs(seed: int=0):
    np.random.seed(seed)
    _w = jnp.asarray

    def _rec_inputs():
        import jax
        import jax.numpy as jnp
        _gk = jax.random.key(seed)
        x = -0.0003713 + 1 * jax.random.normal(jax.random.fold_in(_gk, 1), (6250, 256), jnp.float32)
        _s = jax.random.randint(jax.random.fold_in(_gk, 2), (100000,), 0, 6250, jnp.int32)
        _d = jax.random.randint(jax.random.fold_in(_gk, 3), (100000,), 0, 6250, jnp.int32)
        _loop = jnp.arange(6250, dtype=jnp.int32)
        src = jnp.concatenate([_s, _d, _loop])
        dst = jnp.concatenate([_d, _s, _loop])
        _o = jnp.argsort(dst, stable=True)
        src = src[_o]
        dst = dst[_o]
        edge_attr_65 = 0.000166551 + 1.00014 * jax.random.normal(jax.random.fold_in(_gk, 11), (206250, 65), jnp.float32)
        return (x, src, dst, edge_attr_65)
    x, src, dst, edge_attr_65 = _rec_inputs()

    def _L0_gnn_setup():
        import jax, jax.numpy as jnp
        import numpy as np
        N_NODES = 6250
        N_EDGES = 100000
        D = 256
        F_EDGE = 64
        LN_EPS = 1e-05
        key = jax.random.key(seed)
        ks = jax.random.split(key, 12)
        s = 0.05
        return {'x': jax.random.normal(ks[0], (N_NODES, D), jnp.float32), 'edge_index': jax.random.randint(ks[1], (2, N_EDGES), 0, N_NODES, jnp.int64), 'edge_attr': jax.random.normal(ks[2], (N_EDGES, F_EDGE + 1), jnp.float32), 'W_e1': jax.random.normal(ks[3], (D, F_EDGE), jnp.float32) * s, 'b_e1': jnp.zeros((D,), jnp.float32), 'W_e2': jax.random.normal(ks[4], (D, D), jnp.float32) * s, 'b_e2': jnp.zeros((D,), jnp.float32), 'W_le': jax.random.normal(ks[5], (D, D), jnp.float32) * s, 'b_le': jnp.zeros((D,), jnp.float32), 'W_g1': jax.random.normal(ks[6], (D, D), jnp.float32) * s, 'b_g1': jnp.zeros((D,), jnp.float32), 'ln_g': jnp.ones((D,), jnp.float32), 'ln_b': jnp.zeros((D,), jnp.float32), 'W_g2': jax.random.normal(ks[7], (D, D), jnp.float32) * s, 'b_g2': jnp.zeros((D,), jnp.float32)}
    _L0_gnn_all = _L0_gnn_setup()
    _L0_gnn_in = {k: v for k, v in _L0_gnn_all.items() if k in ('W_e1', 'b_e1', 'W_e2', 'b_e2', 'W_le', 'b_le', 'W_g1', 'b_g1', 'ln_g', 'ln_b', 'W_g2', 'b_g2')}
    del _L0_gnn_all
    return {'x': x, 'src': src, 'dst': dst, 'edge_attr_65': edge_attr_65, 'L0_gnn_W_e1': _L0_gnn_in['W_e1'], 'L0_gnn_b_e1': _L0_gnn_in['b_e1'], 'L0_gnn_W_e2': _L0_gnn_in['W_e2'], 'L0_gnn_b_e2': _L0_gnn_in['b_e2'], 'L0_gnn_W_le': _L0_gnn_in['W_le'], 'L0_gnn_b_le': _L0_gnn_in['b_le'], 'L0_gnn_W_g1': _L0_gnn_in['W_g1'], 'L0_gnn_b_g1': _L0_gnn_in['b_g1'], 'L0_gnn_ln_g': _L0_gnn_in['ln_g'], 'L0_gnn_ln_b': _L0_gnn_in['ln_b'], 'L0_gnn_W_g2': _L0_gnn_in['W_g2'], 'L0_gnn_b_g2': _L0_gnn_in['b_g2']}

def reference(x, src, dst, edge_attr_65, L0_gnn_W_e1, L0_gnn_b_e1, L0_gnn_W_e2, L0_gnn_b_e2, L0_gnn_W_le, L0_gnn_b_le, L0_gnn_W_g1, L0_gnn_b_g1, L0_gnn_ln_g, L0_gnn_ln_b, L0_gnn_W_g2, L0_gnn_b_g2):
    import jax
    import jax.numpy as jnp

    def _L0_gnn_ref(x, edge_index, edge_attr, W_e1, b_e1, W_e2, b_e2, W_le, b_le, W_g1, b_g1, ln_g, ln_b, W_g2, b_g2):
        import jax, jax.numpy as jnp
        import numpy as np
        N_NODES = 6250
        N_EDGES = 100000
        D = 256
        F_EDGE = 64
        LN_EPS = 1e-05
        polarity = jnp.clip(edge_attr[:, 0:1], 0.0, 1.0)
        raw = edge_attr[:, 1:]
        e = jax.nn.relu(raw @ W_e1.T + b_e1) @ W_e2.T + b_e2
        gated = e * (polarity + 0.01)
        edge_emb = gated @ W_le.T + b_le
        src, dst = (edge_index[0], edge_index[1])
        msg = jax.nn.relu(x[src] + edge_emb)
        aggr = jax.ops.segment_sum(msg, dst, num_segments=x.shape[0])
        h = (x + aggr) @ W_g1.T + b_g1
        mu = jnp.mean(h, axis=-1, keepdims=True)
        var = jnp.mean(jnp.square(h - mu), axis=-1, keepdims=True)
        hn = (h - mu) * jax.lax.rsqrt(var + LN_EPS) * ln_g + ln_b
        return jax.nn.relu(hn) @ W_g2.T + b_g2
    edge_index = jnp.stack([src, dst])
    h = jnp.maximum(_layernorm(x, axis=-1), 0.0)
    x = x + _L0_gnn_ref(h, edge_index, edge_attr_65, L0_gnn_W_e1, L0_gnn_b_e1, L0_gnn_W_e2, L0_gnn_b_e2, L0_gnn_W_le, L0_gnn_b_le, L0_gnn_W_g1, L0_gnn_b_g1, L0_gnn_ln_g, L0_gnn_ln_b, L0_gnn_W_g2, L0_gnn_b_g2)
    return x

_drawn_inputs = setup_inputs


def setup_inputs(seed=0):
    import zlib

    import numpy as np

    out = dict(_drawn_inputs(seed))
    spreads = {'L0_gnn_b_e1': (0.0, 2.0),
     'L0_gnn_b_e2': (0.0, 0.445),
     'L0_gnn_b_le': (0.0, 0.1),
     'L0_gnn_b_g1': (0.0, 2.0),
     'L0_gnn_ln_g': (1.0, 0.2),
     'L0_gnn_ln_b': (0.0, 0.1),
     'L0_gnn_b_g2': (0.0, 0.1)}
    factors = {'edge_attr_65': 4.079, 'L0_gnn_W_e1': 4.893}
    for name, (base, spread) in spreads.items():
        noise = np.random.default_rng([zlib.crc32(name.encode()), seed]).standard_normal(out[name].shape)
        drawn = base * np.exp(spread * noise) if base else spread * noise
        out[name] = jnp.asarray(drawn.astype(out[name].dtype))
    for name, factor in factors.items():
        out[name] = (out[name] * factor).astype(out[name].dtype)
    return out
```

```python
import concourse.bass as bass
from concourse import mybir
from contextlib import ExitStack

F32 = mybir.dt.float32
F32R = mybir.dt.float32r
I32 = mybir.dt.int32
ALU = mybir.AluOpType
ACT = mybir.ActivationFunctionType
AX = mybir.AxisListType

N = 6250
E = 206250
D = 256
F = 64
EPS = 1e-05
P = 128
NT = 49
NP = NT * P
LAST = N - (NT - 1) * P
ST = 125
NS = E // ST
NODE_GROUPS = [(4 * g, min(4, NT - 4 * g)) for g in range((NT + 3) // 4)]
X_CHUNKS = [(7 * c, 7) for c in range(6)] + [(42, 6)]


def gnn(nc, x, src, dst, attrT, W_e1T, b_e1, W_e2, b_e2, W_leT, b_le,
        W_g1T, b_g1, ln_g, ln_b, W_g2T, b_g2, out):
    ctx = ExitStack()
    with ctx:
        tables = nc.dram_tensor("gather_table", [NP, D], F32, kind="Internal").ap()
        aggd = nc.dram_tensor("aggregate_table", [NP + P, D], F32, kind="Internal").ap()

        def sb(name, shape, dt=F32, c=ctx):
            return c.enter_context(nc.sbuf_tensor(name, shape, dt))

        def sem(name, c=ctx):
            return c.enter_context(nc.semaphore(name))

        bank = [ctx.enter_context(nc.psum_tensor(f"bank{i}", [P, 512], F32)) for i in range(8)]
        ident = sb("ident", [P, P])
        ones = sb("ones", [P, P])
        iota_i = sb("iota_i", [P, P], I32)
        iota = sb("iota", [P, P])
        x_sb = sb("x_sb", [P, NT, D])
        aggT = sb("aggT", [P, 2, NP])
        w1 = sb("w1", [F, D])
        b1 = sb("b1", [P, 2])
        we2 = sb("we2", [P, 2, D])
        be2 = sb("be2", [P, 2])
        wle = sb("wle", [P, 2, D])
        wc = sb("wc", [P, 2, D])
        c2 = sb("c2", [1, D])
        ble = sb("ble", [P, D])
        wg1 = sb("wg1", [P, 2, D])
        bg1 = sb("bg1", [1, D])
        lng = sb("lng", [P, 2])
        lnb = sb("lnb", [P, 2])
        wg2 = sb("wg2", [P, 2, D])
        bg2 = sb("bg2", [P, D])
        st = sb("st", [P, NT, 6])
        mv = sb("mv", [P, NT, 2])
        rs = sb("rs", [P, NT])

        def setup():
            with ExitStack() as c:
                s_w = sem("s_w", c)
                s_m = sem("s_m", c)
                s_io = sem("s_io", c)
                s_c = sem("s_c", c)
                block = c.enter_context(nc.Block())

                loads = [
                    (w1[:, :], W_e1T), (b1[:, :], b_e1),
                    (we2[:, :, :], W_e2.rearrange("(k p) n -> p k n", p=P)),
                    (be2[:, :], b_e2),
                    (wle[:, :, :], W_leT.rearrange("(k p) n -> p k n", p=P)),
                    (ble[:, :], b_le[None, :].broadcast_to([P, D])),
                    (wg1[:, :, :], W_g1T.rearrange("(k p) n -> p k n", p=P)),
                    (bg1[:, :], b_g1[None, :]),
                    (lng[:, :], ln_g),
                    (lnb[:, :], ln_b),
                    (wg2[:, :, :], W_g2T.rearrange("(k p) n -> p k n", p=P)),
                    (bg2[:, :], b_g2[None, :].broadcast_to([P, D])),
                ]

                @block.sync
                def _(eng):
                    for dst_ap, src_ap in loads:
                        eng.dma_start(dst_ap, src_ap).then_inc(s_w, 16)

                @block.gpsimd
                def _(eng):
                    eng.memset(ident[:, :], 0.0).then_inc(s_m, 1)
                    eng.memset(ones[:, :], 1.0)
                    eng.iota(iota_i[:, :], pattern=[[1, P]], base=0, channel_multiplier=0).then_inc(s_io, 1)
                    eng.wait_ge(s_m, 1)
                    eng.affine_select(out=ident[:, :], in_=ident[:, :], compare_op=ALU.not_equal, fill=1.0,
                                      base=0, pattern=[[-1, P]], channel_multiplier=1)

                @block.tensor
                def _(eng):
                    eng.wait_ge(s_w, 16 * len(loads))
                    for k in range(2):
                        for m in range(2):
                            eng.matmul(bank[0][:, D * k:D * k + D], we2[:, m, P * k:P * k + P], wle[:, m, :],
                                       start=(m == 0), stop=(m == 1))
                    for m in range(2):
                        last = eng.matmul(bank[1][0:1, 0:D], be2[:, m:m + 1], wle[:, m, :],
                                          start=(m == 0), stop=(m == 1))
                    last.then_inc(s_c, 1)

                @block.vector
                def _(eng):
                    eng.wait_ge(s_io, 1)
                    eng.tensor_copy(iota[:, :], iota_i[:, :])
                    eng.wait_ge(s_c, 1)
                    eng.tensor_copy(wc[:, :, :], bank[0][:, :].rearrange("p (k n) -> p k n", k=2))
                    eng.tensor_copy(c2[:, :], bank[1][0:1, 0:D])

        def node_prelude(tag):
            with ExitStack() as c:
                xn = sb(f"xn{tag}", [P, 2, 4, D], F32, c)
                h = sb(f"h{tag}", [P, 2, 4, D], F32, c)
                hb = sb(f"hb{tag}", [P, 2, 4, D], F32, c)
                s_z = sem(f"s_z{tag}", c)
                s_x = [sem(f"s_x{tag}_{i}", c) for i in range(len(X_CHUNKS) + 1)]
                s_st = sem(f"s_st{tag}", c)
                s_ag = sem(f"s_ag{tag}", c)
                s_sq = sem(f"s_sq{tag}", c)
                s_rs = sem(f"s_rs{tag}", c)
                s_n = sem(f"s_n{tag}", c)
                s_h = sem(f"s_h{tag}", c)
                s_hb = sem(f"s_hb{tag}", c)
                s_o = [sem(f"s_o{tag}_{i}", c) for i in range(2)]
                s_t = sem(f"s_t{tag}", c)
                s_e = sem(f"s_e{tag}", c)
                block = c.enter_context(nc.Block())

                @block.sync
                def _(eng):
                    for i, (t, n) in enumerate(X_CHUNKS):
                        eng.dma_start(x_sb[:, t:t + n, :],
                                      x[t * P:(t + n) * P, :].rearrange("(t p) d -> p t d", p=P)).then_inc(s_x[i], 16)
                    eng.wait_ge(s_z, 1)
                    eng.dma_start(x_sb[0:LAST, NT - 1, :], x[(NT - 1) * P:N, :]).then_inc(s_x[-1], 16)
                    for g, (t, n) in enumerate(NODE_GROUPS):
                        eng.wait_ge(s_hb, g + 1)
                        eng.dma_start(tables[t * P:(t + n) * P, :].rearrange("(t p) d -> p t d", p=P),
                                      hb[:, g % 2, 0:n, :]).then_inc(s_o[g % 2], 16)
                    for i in range(2):
                        eng.wait_ge(s_o[i], 16 * len(range(i, len(NODE_GROUPS), 2)))

                @block.vector
                def _(eng):
                    eng.memset(x_sb[96:P, NT - 1, :], 0.0).then_inc(s_z, 1)
                    for i, (t, n) in enumerate(X_CHUNKS + [(NT - 1, 1)]):
                        eng.wait_ge(s_x[i], 16)
                        for k in range(t, t + n):
                            last = eng.bn_stats(st[:, k, :], x_sb[:, k, :])
                    last.then_inc(s_st, 1)
                    eng.wait_ge(s_st, 1)
                    for k in range(NT):
                        last = eng.bn_aggr(mv[:, k, :], st[:, k, :])
                    last.then_inc(s_ag, 1)
                    eng.wait_ge(s_ag, 1)
                    eng.tensor_scalar(rs[:, :], mv[:, :, 1], EPS, None, ALU.add).then_inc(s_ag, 1)
                    eng.wait_ge(s_sq, 1)
                    eng.reciprocal(rs[:, :], rs[:, :]).then_inc(s_rs, 1)
                    eng.wait_ge(s_rs, 1)
                    for g, (t, n) in enumerate(NODE_GROUPS):
                        if g >= 2:
                            eng.wait_ge(s_h, g - 1)
                        for k in range(n):
                            last = eng.tensor_scalar(xn[:, g % 2, k, :], x_sb[:, t + k, :], mv[:, t + k, 0:1],
                                                     rs[:, t + k:t + k + 1], ALU.subtract, ALU.mult)
                        last.then_inc(s_n, 1)

                def evacuate(eng, g):
                    t, n = NODE_GROUPS[g]
                    eng.wait_ge(s_t, g + 1)
                    for k in range(2):
                        last = eng.copy(aggT[:, k, t * P:(t + n) * P], bank[2 * (g % 2) + k][:, 0:n * P])
                    last.then_inc(s_e, 1)

                @block.scalar
                def _(eng):
                    eng.wait_ge(s_ag, 2)
                    eng.activation(rs[:, :], rs[:, :], ACT.Sqrt).then_inc(s_sq, 1)
                    for g, (t, n) in enumerate(NODE_GROUPS):
                        eng.wait_ge(s_n, g + 1)
                        if g >= 2:
                            eng.wait_ge(s_hb, g - 1)
                            eng.wait_ge(s_t, g - 1)
                        eng.activation(h[:, g % 2, 0:n, :], xn[:, g % 2, 0:n, :], ACT.Relu).then_inc(s_h, 1)
                        if g >= 1:
                            evacuate(eng, g - 1)
                    evacuate(eng, len(NODE_GROUPS) - 1)

                @block.gpsimd
                def _(eng):
                    for g, (t, n) in enumerate(NODE_GROUPS):
                        eng.wait_ge(s_h, g + 1)
                        if g >= 2:
                            eng.wait_ge(s_o[g % 2], 16 * (g // 2))
                        for k in range(n):
                            last = eng.tensor_tensor(hb[:, g % 2, k, :], h[:, g % 2, k, :], ble[:, :], ALU.add)
                        last.then_inc(s_hb, 1)

                @block.tensor
                def _(eng):
                    for g, (t, n) in enumerate(NODE_GROUPS):
                        eng.wait_ge(s_h, g + 1)
                        if g >= 2:
                            eng.wait_ge(s_e, g - 1)
                        for j in range(n):
                            for k in range(2):
                                last = eng.transpose(bank[2 * (g % 2) + k][:, j * P:j * P + P],
                                                     h[:, g % 2, j, k * P:k * P + P], ident[:, :])
                        last.then_inc(s_t, 1)

        def general_path(tag):
            with ExitStack() as c:
                zz = sb(f"zz{tag}", [P, 2, D], F32, c)
                raw = sb(f"raw{tag}", [F, ST], F32, c)
                pol = sb(f"pol{tag}", [ST, 1], F32, c)
                gate = sb(f"gate{tag}", [ST, 1], F32, c)
                si = sb(f"si{tag}", [ST, 1], I32, c)
                di = sb(f"di{tag}", [ST, 1], I32, c)
                dbi = sb(f"dbi{tag}", [ST, ST], I32, c)
                df = sb(f"df{tag}", [ST, 1], F32, c)
                dbf = sb(f"dbf{tag}", [ST, ST], F32, c)
                eq = sb(f"eq{tag}", [ST, ST], F32, c)
                low = sb(f"low{tag}", [P, P], F32, c)
                lm = sb(f"lm{tag}", [ST, ST], F32, c)
                cnt = sb(f"cnt{tag}", [ST, 1], F32, c)
                dup = sb(f"dup{tag}", [ST, 1], F32, c)
                tr_i = sb(f"tr_i{tag}", [P, 1], I32, c)
                tr = sb(f"tr{tag}", [P, 1], F32, c)
                dl = sb(f"dl{tag}", [ST, 1], F32, c)
                tf = sb(f"tf{tag}", [ST, 1], F32, c)
                ti = sb(f"ti{tag}", [ST, 1], I32, c)
                hx = sb(f"hx{tag}", [ST, D], F32, c)
                hid = sb(f"hid{tag}", [P, 2, ST], F32, c)
                msg = sb(f"msg{tag}", [ST, D], F32, c)
                msr = sb(f"msr{tag}", [ST, D], F32, c)
                ssum = sb(f"ssum{tag}", [ST, D], F32, c)
                s0 = sem(f"s_g0{tag}", c)
                s1 = sem(f"s_g1{tag}", c)
                s2 = sem(f"s_g2{tag}", c)
                s3 = sem(f"s_g3{tag}", c)
                with nc.Block() as block:
                    @block.vector
                    def _(eng):
                        eng.memset(zz[:, :, :], 0.0).then_inc(s0, 1)
                        eng.wait_ge(s2, 1)
                        eng.tensor_copy(tr[:, :], tr_i[:, :])

                    @block.gpsimd
                    def _(eng):
                        eng.memset(low[:, :], 1.0).then_inc(s1, 1)
                        eng.iota(tr_i[:, :], pattern=[[0, 1]], base=NP, channel_multiplier=1).then_inc(s2, 1)
                        eng.wait_ge(s1, 1)
                        eng.affine_select(out=low[:, :], in_=low[:, :], compare_op=ALU.is_gt, fill=0.0,
                                          base=0, pattern=[[-1, P]], channel_multiplier=1)

                    @block.sync
                    def _(eng):
                        eng.wait_ge(s0, 1)
                        for t in range(0, NT + 1, 2):
                            eng.dma_start(aggd[t * P:(t + 2) * P, :].rearrange("(t p) d -> p t d", p=P),
                                          zz[:, :, :]).then_inc(s3, 16)
                        eng.wait_ge(s3, 16 * len(range(0, NT + 1, 2)))

                sl = sem(f"s_l{tag}", c)
                sg = sem(f"s_ga{tag}", c)
                s_l1 = sem(f"s_l1{tag}", c)
                s_hid = sem(f"s_hid{tag}", c)
                s_l2 = sem(f"s_l2{tag}", c)
                s_v = sem(f"s_v{tag}", c)
                s_ms = sem(f"s_ms{tag}", c)
                s_sum = sem(f"s_sum{tag}", c)
                s_ss = sem(f"s_ss{tag}", c)
                s_sc = sem(f"s_sc{tag}", c)
                every = [sl, s_l1, s_hid, s_l2, s_v, s_ms, s_sum, s_ss]
                with nc.Fori(0, NS) as i:
                    with nc.Block() as block:
                        @block.sync
                        def _(eng):
                            for s in every:
                                eng.sem_clear(s)

                        @block.gpsimd
                        def _(eng):
                            eng.dma_reset(range(sg.num, sg.num + 1))
                            eng.dma_reset(range(s_sc.num, s_sc.num + 1))
                            eng.sem_clear(sg)
                            eng.sem_clear(s_sc)

                    with nc.Block() as block:
                        @block.sync
                        def _(eng):
                            e0 = i * ST
                            eng.dma_start(raw[:, :], attrT[1:1 + F, bass.ds(e0, ST)]).then_inc(sl, 16)
                            eng.dma_start(pol[:, :], attrT[0, bass.ds(e0, ST)][:, None]).then_inc(sl, 16)
                            eng.dma_start(si[:, :], src[bass.ds(e0, ST)][:, None]).then_inc(sl, 16)
                            eng.dma_start(di[:, :], dst[bass.ds(e0, ST)][:, None]).then_inc(sl, 16)
                            eng.dma_start(dbi[:, :], dst[bass.ds(e0, ST)][None, :].broadcast_to([ST, ST])).then_inc(sl, 16)

                        @block.gpsimd
                        def _(eng):
                            eng.wait_ge(sl, 80)
                            eng.indirect_dma_start(out=hx[:, :], out_offset=None, in_=tables,
                                                   in_offset=bass.IndirectOffsetOnAxis(ap=si[:, 0:1], axis=0)).then_inc(sg, 16)
                            eng.wait_ge(s_ss, 1)
                            eng.indirect_dma_start(out=aggd,
                                                   out_offset=bass.IndirectOffsetOnAxis(ap=ti[:, 0:1], axis=0),
                                                   in_=ssum[:, :], in_offset=None, compute_op=ALU.add).then_inc(s_sc, 16)
                            eng.wait_ge(s_sc, 16)

                        @block.tensor
                        def _(eng):
                            eng.wait_ge(sl, 80)
                            for k in range(2):
                                last = eng.matmul(bank[k][:, 0:ST], w1[:, k * P:k * P + P], raw[:, :], start=True, stop=True)
                            last.then_inc(s_l1, 1)
                            eng.wait_ge(s_hid, 1)
                            for k in range(2):
                                eng.matmul(bank[2][0:ST, 0:D], hid[:, k, :], wc[:, k, :], start=(k == 0), stop=False)
                            eng.matmul(bank[2][0:ST, 0:D], ones[0:1, 0:ST], c2[:, :], start=False, stop=True).then_inc(s_l2, 1)
                            eng.wait_ge(s_ms, 1)
                            eng.matmul(bank[3][0:ST, 0:D], eq[:, :], msr[:, :], start=True, stop=True).then_inc(s_sum, 1)

                        @block.scalar
                        def _(eng):
                            eng.wait_ge(s_l1, 1)
                            for k in range(2):
                                last = eng.activation(hid[:, k, :], bank[k][:, 0:ST], ACT.Relu, bias=b1[:, k:k + 1])
                            last.then_inc(s_hid, 1)

                        @block.vector
                        def _(eng):
                            n = [0]

                            def link(ins):
                                n[0] += 1
                                ins.then_inc(s_v, 1)
                                eng.wait_ge(s_v, n[0])

                            eng.wait_ge(sl, 80)
                            link(eng.tensor_scalar(gate[:, :], pol[:, :], 0.0, 1.0, ALU.max, ALU.min))
                            link(eng.tensor_scalar(gate[:, :], gate[:, :], 0.01, None, ALU.add))
                            link(eng.tensor_copy(df[:, :], di[:, :]))
                            link(eng.tensor_copy(dbf[:, :], dbi[:, :]))
                            link(eng.tensor_scalar(eq[:, :], dbf[:, :], df[:, 0:1], None, ALU.is_equal))
                            link(eng.tensor_tensor(lm[:, :], eq[:, :], low[0:ST, 0:ST], ALU.mult))
                            link(eng.tensor_reduce(cnt[:, :], lm[:, :], axis=AX.X, op=ALU.max))
                            link(eng.tensor_tensor(dl[:, :], tr[0:ST, :], df[:, :], ALU.subtract))
                            link(eng.tensor_tensor(dup[:, :], dl[:, :], cnt[:, :], ALU.mult))
                            link(eng.tensor_tensor(tf[:, :], dup[:, :], df[:, :], ALU.add))
                            link(eng.tensor_copy(ti[:, :], tf[:, :]))
                            eng.wait_ge(s_l2, 1)
                            eng.wait_ge(sg, 16)
                            link(eng.scalar_tensor_tensor(out=msg[:, :], in0=bank[2][0:ST, 0:D], scalar=gate[:, 0:1],
                                                          in1=hx[:, :], op0=ALU.mult, op1=ALU.add))
                            eng.tensor_scalar(msr[:, :], msg[:, :], 0.0, None, ALU.max).then_inc(s_ms, 1)
                            eng.wait_ge(s_sum, 1)
                            eng.tensor_copy(ssum[:, :], bank[3][0:ST, 0:D]).then_inc(s_ss, 1)

                ag = sb(f"ag{tag}", [P, 2, D], F32, c)
                s_al = [sem(f"s_al{tag}{i}", c) for i in range(2)]
                s_at = sem(f"s_at{tag}", c)
                s_ad = sem(f"s_ad{tag}", c)
                with nc.Block() as block:
                    @block.sync
                    def _(eng):
                        for t in range(NT):
                            if t >= 2:
                                eng.wait_ge(s_at, t - 1)
                            eng.dma_start(ag[:, t % 2, :], aggd[t * P:(t + 1) * P, :]).then_inc(s_al[t % 2], 16)

                    @block.tensor
                    def _(eng):
                        for t in range(NT):
                            eng.wait_ge(s_al[t % 2], 16 * (t // 2 + 1))
                            if t >= 2:
                                eng.wait_ge(s_ad, t - 1)
                            for k in range(2):
                                last = eng.transpose(bank[t % 2][:, k * P:k * P + P], ag[:, t % 2, k * P:k * P + P], ident[:, :])
                            last.then_inc(s_at, 1)

                    @block.vector
                    def _(eng):
                        for t in range(NT):
                            eng.wait_ge(s_at, t + 1)
                            to = aggT[:, :, t * P:(t + 1) * P]
                            eng.tensor_tensor(to, bank[t % 2][:, 0:2 * P].rearrange("p (k n) -> p k n", k=2), to,
                                              ALU.add).then_inc(s_ad, 1)

        def epilogue():
            with ExitStack() as c:
                g1 = sb("g1", [P, NT, D], F32, c)
                nn = sb("nn", [P, 2, 4, D], F32, c)
                rT = sb("rT", [P, 2, 2, 512], F32, c)
                y = sb("y", [P, 2, 4, D], F32, c)
                s_g1 = sem("e_g1", c)
                s_st = sem("e_st", c)
                s_cp = sem("e_cp", c)
                s_ag = sem("e_ag", c)
                s_sq = sem("e_sq", c)
                s_rs = sem("e_rs", c)
                s_n = sem("e_n", c)
                s_t = sem("e_t", c)
                s_r = sem("e_r", c)
                s_g2 = sem("e_g2", c)
                s_y = sem("e_y", c)
                s_xb = sem("e_xb", c)
                s_o = [sem(f"e_o{i}", c) for i in range(2)]
                block = c.enter_context(nc.Block())

                @block.tensor
                def _(eng):
                    for t in range(NT):
                        if t >= 4:
                            eng.wait_ge(s_cp, t - 3)
                        o = bank[t % 4][:, 0:D]
                        for k in range(2):
                            eng.matmul(o, aggT[:, k, t * P:(t + 1) * P], wg1[:, k, :], start=(k == 0), stop=False)
                        eng.matmul(o, ones[0:1, :], bg1[:, :], start=False, stop=True).then_inc(s_g1, 1)

                    def down(g):
                        t, n = NODE_GROUPS[g]
                        eng.wait_ge(s_r, g + 1)
                        for j in range(n):
                            q = t + j
                            if q >= 4:
                                eng.wait_ge(s_y, q - 3)
                            for k in range(2):
                                last = eng.matmul(bank[4 + q % 4][:, 0:D], rT[:, g % 2, k, j * P:j * P + P],
                                                  wg2[:, k, :], start=(k == 0), stop=(k == 1))
                            last.then_inc(s_g2, 1)

                    eng.wait_ge(s_cp, NT)
                    for g, (t, n) in enumerate(NODE_GROUPS):
                        eng.wait_ge(s_n, g + 1)
                        if g >= 2:
                            eng.wait_ge(s_r, g - 1)
                        for j in range(n):
                            for k in range(2):
                                last = eng.transpose(bank[2 * (g % 2) + k][:, j * P:j * P + P],
                                                     nn[:, g % 2, j, k * P:k * P + P], ident[:, :])
                        last.then_inc(s_t, 1)
                        if g >= 1:
                            down(g - 1)
                    down(len(NODE_GROUPS) - 1)

                @block.vector
                def _(eng):
                    for t in range(NT):
                        eng.wait_ge(s_cp, t + 1)
                        eng.bn_stats(st[:, t, :], g1[:, t, :]).then_inc(s_st, 1)
                    eng.wait_ge(s_st, NT)
                    for t in range(NT):
                        last = eng.bn_aggr(mv[:, t, :], st[:, t, :])
                    last.then_inc(s_ag, 1)
                    eng.wait_ge(s_ag, 1)
                    eng.tensor_scalar(rs[:, :], mv[:, :, 1], EPS, None, ALU.add).then_inc(s_ag, 1)
                    eng.wait_ge(s_sq, 1)
                    eng.reciprocal(rs[:, :], rs[:, :]).then_inc(s_rs, 1)
                    eng.wait_ge(s_rs, 1)

                    def finish(g):
                        t, n = NODE_GROUPS[g]
                        if g >= 2:
                            eng.wait_ge(s_o[g % 2], 16 * (g // 2))
                        for j in range(n):
                            eng.wait_ge(s_xb, t + j + 1)
                            eng.wait_ge(s_g2, t + j + 1)
                            eng.tensor_tensor(y[:, g % 2, j, :], bank[4 + (t + j) % 4][:, 0:D], x_sb[:, t + j, :],
                                              ALU.add).then_inc(s_y, 1)

                    for g, (t, n) in enumerate(NODE_GROUPS):
                        if g >= 2:
                            eng.wait_ge(s_t, g - 1)
                        for j in range(n):
                            last = eng.tensor_scalar(nn[:, g % 2, j, :], g1[:, t + j, :], mv[:, t + j, 0:1],
                                                     rs[:, t + j:t + j + 1], ALU.subtract, ALU.mult)
                        last.then_inc(s_n, 1)
                        if g >= 2:
                            finish(g - 2)
                    finish(len(NODE_GROUPS) - 2)
                    finish(len(NODE_GROUPS) - 1)

                @block.gpsimd
                def _(eng):
                    for t in range(NT):
                        eng.tensor_tensor(x_sb[:, t, :], x_sb[:, t, :], bg2[:, :], ALU.add).then_inc(s_xb, 1)

                @block.scalar
                def _(eng):
                    for t in range(NT):
                        eng.wait_ge(s_g1, t + 1)
                        eng.copy(g1[:, t, :], bank[t % 4][:, 0:D]).then_inc(s_cp, 1)
                    eng.wait_ge(s_ag, 2)
                    eng.activation(rs[:, :], rs[:, :], ACT.Sqrt).then_inc(s_sq, 1)
                    for g, (t, n) in enumerate(NODE_GROUPS):
                        eng.wait_ge(s_t, g + 1)
                        if g >= 2:
                            tt, m = NODE_GROUPS[g - 2]
                            eng.wait_ge(s_g2, tt + m)
                        for k in range(2):
                            last = eng.activation(rT[:, g % 2, k, 0:n * P], bank[2 * (g % 2) + k][:, 0:n * P], ACT.Relu,
                                                  bias=lnb[:, k:k + 1], scale=lng[:, k:k + 1])
                        last.then_inc(s_r, 1)

                @block.sync
                def _(eng):
                    for g, (t, n) in enumerate(NODE_GROUPS):
                        eng.wait_ge(s_y, t + n)
                        if t + n < NT:
                            eng.dma_start(out[t * P:(t + n) * P, :].rearrange("(t p) d -> p t d", p=P),
                                          y[:, g % 2, 0:n, :]).then_inc(s_o[g % 2], 16)
                        else:
                            eng.dma_start(out[t * P:N, :], y[0:LAST, g % 2, 0, :]).then_inc(s_o[g % 2], 16)
                    for i in range(2):
                        eng.wait_ge(s_o[i], 16 * len(range(i, len(NODE_GROUPS), 2)))

        setup()
        node_prelude("a")
        general_path("a")
        epilogue()


def kernel(**inputs):
    import numpy as _np
    import concourse.bacc as _bacc
    from concourse import mybir as _mybir
    from concourse.bass_utils import run_bass_kernel_spmd as _run

    w = {k: _np.asarray(v) for k, v in inputs.items()}
    p = "L0_gnn_"
    data = [
        ("x", w["x"]), ("src", w["src"]), ("dst", w["dst"]),
        ("attrT", _np.ascontiguousarray(w["edge_attr_65"].T)),
        ("W_e1T", _np.ascontiguousarray(w[p + "W_e1"].T)), ("b_e1", w[p + "b_e1"].reshape(2, P).T),
        ("W_e2", w[p + "W_e2"]), ("b_e2", w[p + "b_e2"].reshape(2, P).T),
        ("W_leT", _np.ascontiguousarray(w[p + "W_le"].T)), ("b_le", w[p + "b_le"]),
        ("W_g1T", _np.ascontiguousarray(w[p + "W_g1"].T)), ("b_g1", w[p + "b_g1"]),
        ("ln_g", w[p + "ln_g"].reshape(2, P).T), ("ln_b", w[p + "ln_b"].reshape(2, P).T),
        ("W_g2T", _np.ascontiguousarray(w[p + "W_g2"].T)), ("b_g2", w[p + "b_g2"]),
    ]
    nc = _bacc.Bacc("TRN2", target_bir_lowering=False, num_devices=1)
    arrays, args = {}, []
    for name, a in data:
        a = _np.ascontiguousarray(a)
        arrays[f"in_{name}"] = a
        args.append(nc.dram_tensor(f"in_{name}", a.shape, _mybir.dt.from_np(a.dtype), kind="ExternalInput").ap())
    o = nc.dram_tensor("out_0", (N, D), _mybir.dt.float32, kind="ExternalOutput").ap()
    gnn(nc, *args, o)
    r = _run(nc, [arrays], core_ids=[0])
    return r.results[0]["out_0"]
```

```python
import concourse.bass as bass
from concourse import mybir
from contextlib import ExitStack

F32 = mybir.dt.float32
F32R = mybir.dt.float32r
I32 = mybir.dt.int32
ALU = mybir.AluOpType
ACT = mybir.ActivationFunctionType
AX = mybir.AxisListType

N = 6250
E = 206250
D = 256
F = 64
EPS = 1e-05
P = 128
NT = 49
NP = NT * P
LAST = N - (NT - 1) * P
ST = 125
NS = E // ST
TILES = (E + P - 1) // P
FULL = E // P
TAIL = E - FULL * P
UNITS = TILES // 4
GU = 4
GROUPS = (UNITS + GU - 1) // GU
GE = GU * 4 * P
TOP = NP - P
NR = 3
NX = 4
NODE_GROUPS = [(4 * g, min(4, NT - 4 * g)) for g in range((NT + 3) // 4)]
X_CHUNKS = [(7 * c, 7) for c in range(6)] + [(42, 6)]


def gnn(nc, x, src, dst, src_m, dst_m, pol_m, pol, first, attrT, W_e1T, b_e1, b_e1r, W_e2, b_e2, W_leT, b_le,
        W_g1T, b_g1, ln_g, ln_b, W_g2T, b_g2, out):
    ctx = ExitStack()
    with ctx:
        tables = nc.dram_tensor("gather_table", [NP, D], F32, kind="Internal").ap()
        aggd = nc.dram_tensor("aggregate_table", [NP + P, D], F32, kind="Internal").ap()

        def sb(name, shape, dt=F32, c=ctx):
            return c.enter_context(nc.sbuf_tensor(name, shape, dt))

        def sem(name, c=ctx):
            return c.enter_context(nc.semaphore(name))

        bank = [ctx.enter_context(nc.psum_tensor(f"bank{i}", [P, 512], F32)) for i in range(8)]
        ident = sb("ident", [P, P])
        ones = sb("ones", [P, P])
        iota_i = sb("iota_i", [P, P], I32)
        iota = sb("iota", [P, P])
        aggT = sb("aggT", [P, 2, NP])
        w1 = sb("w1", [P, D])
        w1r = sb("w1r", [P, 2, D], F32R)
        btmp = sb("btmp", [P, D])
        btmr = sb("btmr", [P, D], F32R)
        wcr = sb("wcr", [P, 2, 2, D], F32R)
        c2r = sb("c2r", [P, D], F32R)
        onr = sb("onr", [P, P], F32R)
        sidx = sb("sidx", [P, TILES], I32)
        slot = sb("slot", [P, TILES])
        gt = sb("gt", [P, TILES])
        base = sb("base", [P, GROUPS])
        base_i = sb("base_i", [1, GROUPS], I32)
        flag_i = sb("flag_i", [1, 1], I32)
        b1 = sb("b1", [P, 2])
        we2 = sb("we2", [P, 2, D])
        be2 = sb("be2", [P, 2])
        wle = sb("wle", [P, 2, D])
        wc = sb("wc", [P, 2, D])
        c2 = sb("c2", [1, D])
        ble = sb("ble", [P, D])
        wg1 = sb("wg1", [P, 2, D])
        bg1 = sb("bg1", [1, D])
        lng = sb("lng", [P, 2])
        lnb = sb("lnb", [P, 2])
        wg2 = sb("wg2", [P, 2, D])
        bg2 = sb("bg2", [P, D])
        st = sb("st", [P, NT, 6])
        mv = sb("mv", [P, NT, 2])
        rs = sb("rs", [P, NT])

        def setup():
            with ExitStack() as c:
                dst_i = sb("dst_i", [P, TILES], I32, c)
                first_i = sb("first_i", [P, GROUPS], I32, c)
                low2 = sb("low2", [P, 4], F32, c)
                bad = sb("bad", [P, 1], F32, c)
                s_w = sem("s_w", c)
                s_i = sem("s_i", c)
                s_m = sem("s_m", c)
                s_io = sem("s_io", c)
                s_z = sem("s_zp", c)
                s_c = sem("s_c", c)
                s_v = sem("s_v", c)
                s_bad = sem("s_bad", c)
                s_f = sem("s_f", c)
                block = c.enter_context(nc.Block())

                loads = [
                    (w1[0:F, :], W_e1T), (w1[F:P, :], W_e1T),
                    (btmp[64:65, :], b_e1r[None, :]), (btmp[96:97, :], b_e1r[None, :]),
                    (b1[:, :], b_e1),
                    (we2[:, :, :], W_e2.rearrange("(k p) n -> p k n", p=P)),
                    (be2[:, :], b_e2),
                    (wle[:, :, :], W_leT.rearrange("(k p) n -> p k n", p=P)),
                    (ble[:, :], b_le[None, :].broadcast_to([P, D])),
                    (wg1[:, :, :], W_g1T.rearrange("(k p) n -> p k n", p=P)),
                    (bg1[:, :], b_g1[None, :]),
                    (lng[:, :], ln_g),
                    (lnb[:, :], ln_b),
                    (wg2[:, :, :], W_g2T.rearrange("(k p) n -> p k n", p=P)),
                    (bg2[:, :], b_g2[None, :].broadcast_to([P, D])),
                ]
                edges = [
                    (dst_i[:, 0:FULL], dst_m), (dst_i[0:TAIL, FULL:TILES], dst[FULL * P:E][:, None]),
                    (sidx[:, 0:FULL], src_m), (sidx[0:TAIL, FULL:TILES], src[FULL * P:E][:, None]),
                    (gt[:, 0:FULL], pol_m), (gt[0:TAIL, FULL:TILES], pol[FULL * P:E][:, None]),
                    (first_i[:, :], first[None, :].broadcast_to([P, GROUPS])),
                ]

                @block.sync
                def _(eng):
                    for dst_ap, src_ap in loads:
                        eng.dma_start(dst_ap, src_ap).then_inc(s_w, 16)

                @block.scalar
                def _(eng):
                    eng.wait_ge(s_z, 3)
                    for dst_ap, src_ap in edges:
                        eng.dma_start(dst_ap, src_ap).then_inc(s_i, 16)

                @block.gpsimd
                def _(eng):
                    eng.memset(dst_i[:, FULL:TILES], 0).then_inc(s_z, 1)
                    eng.memset(sidx[:, FULL:TILES], 0).then_inc(s_z, 1)
                    eng.memset(gt[:, FULL:TILES], 0.0).then_inc(s_z, 1)
                    eng.memset(ident[:, :], 0.0).then_inc(s_m, 1)
                    eng.memset(ones[:, :], 1.0)
                    eng.memset(onr[:, :].bitcast(F32), 1.0)
                    eng.memset(c2r[:, :].bitcast(F32), 0.0)
                    eng.memset(w1r[:, 1, :].bitcast(F32), 0.0).then_inc(s_m, 1)
                    eng.iota(iota_i[:, :], pattern=[[1, P]], base=0, channel_multiplier=0).then_inc(s_io, 1)
                    eng.wait_ge(s_m, 1)
                    eng.affine_select(out=ident[:, :], in_=ident[:, :], compare_op=ALU.not_equal, fill=1.0,
                                      base=0, pattern=[[-1, P]], channel_multiplier=1)

                @block.tensor
                def _(eng):
                    eng.wait_ge(s_w, 16 * len(loads))
                    for k in range(2):
                        for m in range(2):
                            eng.matmul(bank[0][:, D * k:D * k + D], we2[:, m, P * k:P * k + P], wle[:, m, :],
                                       start=(m == 0), stop=(m == 1))
                    for m in range(2):
                        last = eng.matmul(bank[1][0:1, 0:D], be2[:, m:m + 1], wle[:, m, :],
                                          start=(m == 0), stop=(m == 1))
                    last.then_inc(s_c, 1)
                    eng.wait_ge(s_bad, 1)
                    eng.wait_ge(s_m, 2)
                    eng.matmul(bank[2][0:1, 0:1], bad[:, 0:1], ones[:, 0:1], start=True, stop=True).then_inc(s_f, 1)

                @block.vector
                def _(eng):
                    n = [0]

                    def link(ins):
                        n[0] += 1
                        ins.then_inc(s_v, 1)
                        eng.wait_ge(s_v, n[0])

                    eng.wait_ge(s_io, 1)
                    eng.tensor_copy(iota[:, :], iota_i[:, :])
                    eng.memset(low2[:, :], 0.0)
                    eng.wait_ge(s_i, 16 * len(edges))
                    eng.tensor_copy(base[:, :], first_i[:, :])
                    eng.tensor_copy(slot[:, :], dst_i[:, :])
                    link(eng.tensor_scalar(gt[:, :], gt[:, :], 0.0, 1.0, ALU.max, ALU.min))
                    link(eng.tensor_scalar(gt[:, :], gt[:, :], 0.01, None, ALU.add))
                    link(eng.tensor_scalar(base[:, :], base[:, :], float(TOP), None, ALU.min))
                    eng.tensor_copy(base_i[:, :], base[0:1, :])
                    w = 4 * GU
                    m = FULL // w
                    sv = slot[:, 0:m * w].rearrange("p (g k) -> p g k", k=w)
                    bv = base[:, 0:m].rearrange("p (g k) -> p g k", k=1).broadcast_to([P, m, w])
                    eng.tensor_tensor(sv, sv, bv, ALU.subtract)
                    link(eng.tensor_scalar(slot[:, m * w:TILES], slot[:, m * w:TILES], base[:, m:m + 1], None, ALU.subtract))
                    eng.tensor_reduce(low2[:, 0:1], slot[:, 0:FULL], axis=AX.X, op=ALU.max)
                    eng.tensor_reduce(low2[:, 1:2], slot[:, 0:FULL], axis=AX.X, op=ALU.min)
                    eng.tensor_copy(low2[0:TAIL, 2:3], slot[0:TAIL, FULL:TILES])
                    link(eng.tensor_copy(low2[0:TAIL, 3:4], slot[0:TAIL, FULL:TILES]))
                    link(eng.tensor_scalar(low2[:, 0:4:2], low2[:, 0:4:2], float(P - 1), None, ALU.is_gt))
                    link(eng.tensor_scalar(low2[:, 1:4:2], low2[:, 1:4:2], 0.0, None, ALU.is_lt))
                    eng.tensor_reduce(bad[:, 0:1], low2[:, :], axis=AX.X, op=ALU.max).then_inc(s_bad, 1)
                    eng.wait_ge(s_c, 1)
                    eng.wait_ge(s_m, 2)
                    link(eng.tensor_copy(wc[:, :, :], bank[0][:, :].rearrange("p (k n) -> p k n", k=2)))
                    link(eng.tensor_copy(c2[:, :], bank[1][0:1, 0:D]))
                    eng.tensor_copy(c2r[0:1, :], c2[:, :])
                    eng.tensor_copy(wcr[:, 0, :, :], wc[:, :, :])
                    eng.tensor_copy(w1r[:, 0, :], w1[:, :])
                    link(eng.tensor_copy(btmr[64:65, :], btmp[64:65, :]))
                    link(eng.tensor_copy(btmr[96:97, :], btmp[96:97, :]))
                    eng.tensor_tensor(c2r[32:33, :], c2[:, :], c2r[0:1, :].bitcast(F32), ALU.subtract)
                    eng.tensor_tensor(wcr[:, 1, :, :], wc[:, :, :], wcr[:, 0, :, :].bitcast(F32), ALU.subtract)
                    eng.tensor_tensor(w1r[0:F, 1, :], w1[0:F, :], w1r[0:F, 0, :].bitcast(F32), ALU.subtract)
                    eng.tensor_copy(w1r[64:65, 1, :], btmp[64:65, :])
                    eng.tensor_tensor(w1r[96:97, 1, :], btmp[96:97, :], btmr[96:97, :].bitcast(F32), ALU.subtract)
                    eng.wait_ge(s_f, 1)
                    eng.tensor_copy(flag_i[:, :], bank[2][0:1, 0:1])

        def node_prelude(tag):
            with ExitStack() as c:
                x_sb = sb(f"x_sb{tag}", [P, NT, D], F32, c)
                xn = sb(f"xn{tag}", [P, 2, 4, D], F32, c)
                h = sb(f"h{tag}", [P, 2, 4, D], F32, c)
                hb = sb(f"hb{tag}", [P, 2, 4, D], F32, c)
                s_z = sem(f"s_z{tag}", c)
                s_x = [sem(f"s_x{tag}_{i}", c) for i in range(len(X_CHUNKS) + 1)]
                s_st = sem(f"s_st{tag}", c)
                s_ag = sem(f"s_ag{tag}", c)
                s_sq = sem(f"s_sq{tag}", c)
                s_rs = sem(f"s_rs{tag}", c)
                s_n = sem(f"s_n{tag}", c)
                s_h = sem(f"s_h{tag}", c)
                s_hb = sem(f"s_hb{tag}", c)
                s_o = [sem(f"s_o{tag}_{i}", c) for i in range(2)]
                s_t = sem(f"s_t{tag}", c)
                s_e = sem(f"s_e{tag}", c)
                block = c.enter_context(nc.Block())

                @block.sync
                def _(eng):
                    for i, (t, n) in enumerate(X_CHUNKS):
                        eng.dma_start(x_sb[:, t:t + n, :],
                                      x[t * P:(t + n) * P, :].rearrange("(t p) d -> p t d", p=P)).then_inc(s_x[i], 16)
                    eng.wait_ge(s_z, 1)
                    eng.dma_start(x_sb[0:LAST, NT - 1, :], x[(NT - 1) * P:N, :]).then_inc(s_x[-1], 16)
                    for g, (t, n) in enumerate(NODE_GROUPS):
                        eng.wait_ge(s_hb, g + 1)
                        eng.dma_start(tables[t * P:(t + n) * P, :].rearrange("(t p) d -> p t d", p=P),
                                      hb[:, g % 2, 0:n, :]).then_inc(s_o[g % 2], 16)
                    for i in range(2):
                        eng.wait_ge(s_o[i], 16 * len(range(i, len(NODE_GROUPS), 2)))

                @block.vector
                def _(eng):
                    eng.memset(x_sb[96:P, NT - 1, :], 0.0).then_inc(s_z, 1)
                    for i, (t, n) in enumerate(X_CHUNKS + [(NT - 1, 1)]):
                        eng.wait_ge(s_x[i], 16)
                        for k in range(t, t + n):
                            last = eng.bn_stats(st[:, k, :], x_sb[:, k, :])
                    last.then_inc(s_st, 1)
                    eng.wait_ge(s_st, 1)
                    for k in range(NT):
                        last = eng.bn_aggr(mv[:, k, :], st[:, k, :])
                    last.then_inc(s_ag, 1)
                    eng.wait_ge(s_ag, 1)
                    eng.tensor_scalar(rs[:, :], mv[:, :, 1], EPS, None, ALU.add).then_inc(s_ag, 1)
                    eng.wait_ge(s_sq, 1)
                    eng.reciprocal(rs[:, :], rs[:, :]).then_inc(s_rs, 1)
                    eng.wait_ge(s_rs, 1)
                    for g, (t, n) in enumerate(NODE_GROUPS):
                        if g >= 2:
                            eng.wait_ge(s_h, g - 1)
                        for k in range(n):
                            last = eng.tensor_scalar(xn[:, g % 2, k, :], x_sb[:, t + k, :], mv[:, t + k, 0:1],
                                                     rs[:, t + k:t + k + 1], ALU.subtract, ALU.mult)
                        last.then_inc(s_n, 1)

                def evacuate(eng, g):
                    t, n = NODE_GROUPS[g]
                    eng.wait_ge(s_t, g + 1)
                    for k in range(2):
                        last = eng.copy(aggT[:, k, t * P:(t + n) * P], bank[2 * (g % 2) + k][:, 0:n * P])
                    last.then_inc(s_e, 1)

                @block.scalar
                def _(eng):
                    eng.wait_ge(s_ag, 2)
                    eng.activation(rs[:, :], rs[:, :], ACT.Sqrt).then_inc(s_sq, 1)
                    for g, (t, n) in enumerate(NODE_GROUPS):
                        eng.wait_ge(s_n, g + 1)
                        if g >= 2:
                            eng.wait_ge(s_hb, g - 1)
                            eng.wait_ge(s_t, g - 1)
                        eng.activation(h[:, g % 2, 0:n, :], xn[:, g % 2, 0:n, :], ACT.Relu).then_inc(s_h, 1)
                        if g >= 1:
                            evacuate(eng, g - 1)
                    evacuate(eng, len(NODE_GROUPS) - 1)

                @block.gpsimd
                def _(eng):
                    for g, (t, n) in enumerate(NODE_GROUPS):
                        eng.wait_ge(s_h, g + 1)
                        if g >= 2:
                            eng.wait_ge(s_o[g % 2], 16 * (g // 2))
                        for k in range(n):
                            last = eng.tensor_tensor(hb[:, g % 2, k, :], h[:, g % 2, k, :], ble[:, :], ALU.add)
                        last.then_inc(s_hb, 1)

                @block.tensor
                def _(eng):
                    for g, (t, n) in enumerate(NODE_GROUPS):
                        eng.wait_ge(s_h, g + 1)
                        if g >= 2:
                            eng.wait_ge(s_e, g - 1)
                        for j in range(n):
                            for k in range(2):
                                last = eng.transpose(bank[2 * (g % 2) + k][:, j * P:j * P + P],
                                                     h[:, g % 2, j, k * P:k * P + P], ident[:, :])
                        last.then_inc(s_t, 1)

        def edge_path():
            with ExitStack() as c:
                raw = sb("raw", [F, NR, 1024], F32, c)
                m1 = sb("m1", [P, 2, 512], F32R, c)
                m2 = sb("m2", [P, 2, 512], F32R, c)
                hh = sb("hh", [P, 2, 2, 512], F32R, c)
                hl = sb("hl", [P, 2, 2, 512], F32R, c)
                hx = sb("hx", [P, NX, 4, D], F32, c)
                mh = sb("mh", [P, 2, 4, D], F32R, c)
                ml = sb("ml", [P, 2, 4, D], F32R, c)
                oh = sb("oh", [P, 2, 4, P], F32R, c)
                agw = sb("agw", [P, 2, D], F32, c)
                r_load = [sem(f"r_load{i}", c) for i in range(NR)]
                r_hx = [sem(f"r_hx{i}", c) for i in range(NX)]
                r_m2 = sem("r_m2", c)
                r_rh = sem("r_rh", c)
                r_rl = sem("r_rl", c)
                r_l1 = sem("r_l1", c)
                r_hh = sem("r_hh", c)
                r_hl = sem("r_hl", c)
                r_l2 = sem("r_l2", c)
                r_t = sem("r_t", c)
                r_mh = sem("r_mh", c)
                r_ml = sem("r_ml", c)
                r_oh = sem("r_oh", c)
                r_sg = sem("r_sg", c)
                r_ev = sem("r_ev", c)
                r_tr = sem("r_tr", c)
                r_ad = sem("r_ad", c)
                LA = [bank[0], bank[1]]
                LB = [bank[2], bank[3], bank[4], bank[5]]
                SG = [bank[6], bank[7]]
                block = c.enter_context(nc.Block())

                @block.sync
                def _(eng):
                    for n in range((UNITS + 1) // 2):
                        if n >= NR:
                            eng.wait_ge(r_rh, 2 * (n - NR) + 2)
                            eng.wait_ge(r_rl, 2 * (n - NR) + 2)
                        w = min(1024, E - 1024 * n)
                        eng.dma_start(raw[:, n % NR, 0:w], attrT[1:1 + F, 1024 * n:1024 * n + w]).then_inc(r_load[n % NR], 16)

                @block.gpsimd
                def _(eng):
                    for u in range(UNITS):
                        if u >= NX:
                            eng.wait_ge(r_t, 2 * (u - NX) + 2)
                        for j in range(4):
                            t = 4 * u + j
                            eng.indirect_dma_start(out=hx[:, u % NX, j, :], out_offset=None, in_=tables,
                                                   in_offset=bass.IndirectOffsetOnAxis(ap=sidx[:, t:t + 1], axis=0)
                                                   ).then_inc(r_hx[u % NX], 16)

                def part(u):
                    return raw[:, (u // 2) % NR, 512 * (u % 2):512 * (u % 2) + 512]

                def loaded(eng, u):
                    eng.wait_ge(r_load[(u // 2) % NR], 16 * ((u // 2) // NR + 1))

                @block.scalar
                def _(eng):
                    def raw_high(u):
                        loaded(eng, u)
                        if u >= 2:
                            eng.wait_ge(r_l1, 2 * (u - 2) + 2)
                        eng.copy(m1[0:F, u % 2, :], part(u))
                        eng.copy(m2[0:F, u % 2, :], part(u)).then_inc(r_rh, 1)

                    def hidden_high(u):
                        if u >= 2:
                            eng.wait_ge(r_l2, 2 * (u - 2) + 2)
                        for k in range(2):
                            eng.wait_ge(r_l1, 2 * u + k + 1)
                            eng.activation(hh[:, u % 2, k, :], LA[k][:, :], ACT.Relu).then_inc(r_hh, 1)

                    def message_high(u):
                        if u >= 2:
                            eng.wait_ge(r_sg, u - 1)
                        for q in range(2):
                            eng.wait_ge(r_t, 2 * u + q + 1)
                            eng.activation(mh[:, u % 2, 2 * q:2 * q + 2, :],
                                           LB[(2 * u + q) % 4][:, :].rearrange("p (j n) -> p j n", j=2),
                                           ACT.Relu).then_inc(r_mh, 1)

                    def window_out(g):
                        eng.wait_ge(r_sg, min(GU * g + GU, UNITS))
                        if g >= 2:
                            eng.wait_ge(r_tr, g - 1)
                        eng.copy(agw[:, g % 2, :], SG[g % 2][:, 0:D]).then_inc(r_ev, 1)

                    raw_high(0)
                    raw_high(1)
                    hidden_high(0)
                    for u in range(UNITS):
                        if u + 1 < UNITS:
                            hidden_high(u + 1)
                        if u + 2 < UNITS:
                            raw_high(u + 2)
                        message_high(u)
                        if u % GU == 0 and u >= GU:
                            window_out(u // GU - 1)
                    window_out(GROUPS - 1)

                @block.vector
                def _(eng):
                    def raw_low(u):
                        loaded(eng, u)
                        eng.wait_ge(r_rh, u + 1)
                        eng.tensor_tensor(m1[F:P, u % 2, :], part(u), m1[0:F, u % 2, :].bitcast(F32),
                                          ALU.subtract).then_inc(r_rl, 1)

                    def hidden_low(u):
                        if u >= 2:
                            eng.wait_ge(r_l2, 2 * (u - 2) + 2)
                        for k in range(2):
                            eng.wait_ge(r_hh, 2 * u + k + 1)
                            eng.scalar_tensor_tensor(out=hl[:, u % 2, k, :], in0=LA[k][:, :], scalar=0.0,
                                                     in1=hh[:, u % 2, k, :].bitcast(F32),
                                                     op0=ALU.max, op1=ALU.subtract).then_inc(r_hl, 1)

                    def onehot(u):
                        if u >= 2:
                            eng.wait_ge(r_sg, u - 1)
                        for j in range(4):
                            t = 4 * u + j
                            last = eng.tensor_scalar(oh[:, u % 2, j, :], iota[:, :], slot[:, t:t + 1], None, ALU.is_equal)
                        last.then_inc(r_oh, 1)

                    def total(u):
                        eng.wait_ge(r_hx[u % NX], 64 * (u // NX + 1))
                        for q in range(2):
                            eng.wait_ge(r_l2, 2 * u + q + 1)
                            for j in range(2):
                                t = 4 * u + 2 * q + j
                                b = LB[(2 * u + q) % 4][:, D * j:D * j + D]
                                last = eng.scalar_tensor_tensor(out=b, in0=b, scalar=gt[:, t:t + 1],
                                                                in1=hx[:, u % NX, 2 * q + j, :],
                                                                op0=ALU.mult, op1=ALU.add)
                            last.then_inc(r_t, 1)

                    def message_low(u):
                        if u >= 2:
                            eng.wait_ge(r_sg, u - 1)
                        for q in range(2):
                            eng.wait_ge(r_mh, 2 * u + q + 1)
                            eng.scalar_tensor_tensor(out=ml[:, u % 2, 2 * q:2 * q + 2, :].rearrange("p j n -> p (j n)"),
                                                     in0=LB[(2 * u + q) % 4][:, :], scalar=0.0,
                                                     in1=mh[:, u % 2, 2 * q:2 * q + 2, :].rearrange("p j n -> p (j n)").bitcast(F32),
                                                     op0=ALU.max, op1=ALU.subtract).then_inc(r_ml, 1)

                    def window_add(g):
                        b0 = eng.value_load(base_i[0:1, g:g + 1], min_val=0, max_val=TOP)
                        eng.wait_ge(r_tr, g + 1)
                        if g >= 1:
                            eng.wait_ge(r_ad, g)
                        to = aggT[:, :, bass.ds(b0, P)]
                        eng.tensor_tensor(to, to, SG[g % 2][:, 0:2 * P].rearrange("p (k n) -> p k n", k=2),
                                          ALU.add).then_inc(r_ad, 1)

                    eng.memset(m2[64:P, :, :].bitcast(F32), 0.0).then_inc(r_m2, 1)
                    eng.wait_ge(r_m2, 1)
                    eng.memset(m2[64:65, :, :].bitcast(F32), 1.0)
                    eng.memset(m2[96:97, :, :].bitcast(F32), 1.0).then_inc(r_m2, 1)
                    raw_low(0)
                    raw_low(1)
                    hidden_low(0)
                    for u in range(UNITS):
                        if u + 1 < UNITS:
                            hidden_low(u + 1)
                        if u + 2 < UNITS:
                            raw_low(u + 2)
                        onehot(u)
                        total(u)
                        message_low(u)
                        if u % GU == 2 and u >= GU:
                            window_add(u // GU - 1)
                    if (UNITS - 1) % GU < 2:
                        window_add(GROUPS - 2)
                    window_add(GROUPS - 1)

                @block.tensor
                def _(eng):
                    def first_layer(u):
                        eng.wait_ge(r_rl, u + 1)
                        if u == 0:
                            eng.wait_ge(r_m2, 2)
                        for k in range(2):
                            if u >= 1:
                                eng.wait_ge(r_hl, 2 * (u - 1) + k + 1)
                            eng.matmul(LA[k][:, :], w1r[:, 0, k * P:k * P + P], m1[:, u % 2, :], start=True, stop=False)
                            eng.matmul(LA[k][:, :], w1r[:, 1, k * P:k * P + P], m2[:, u % 2, :],
                                       start=False, stop=True).then_inc(r_l1, 1)

                    def second_layer(u):
                        eng.wait_ge(r_hh, 2 * u + 2)
                        eng.wait_ge(r_hl, 2 * u + 2)
                        for q in range(2):
                            if u >= 2:
                                eng.wait_ge(r_ml, 2 * (u - 2) + q + 1)
                            for j in range(2):
                                o = LB[(2 * u + q) % 4][:, D * j:D * j + D]
                                e0 = (2 * q + j) * P
                                eng.matmul(o, onr[:, :], c2r[:, :], start=True, stop=False)
                                for k in range(2):
                                    eng.matmul(o, hh[:, u % 2, k, e0:e0 + P], wcr[:, 0, k, :], start=False, stop=False)
                                    eng.matmul(o, hh[:, u % 2, k, e0:e0 + P], wcr[:, 1, k, :], start=False, stop=False)
                                    last = eng.matmul(o, hl[:, u % 2, k, e0:e0 + P], wcr[:, 0, k, :],
                                                      start=False, stop=(k == 1))
                            last.then_inc(r_l2, 1)

                    def segment(u):
                        g = u // GU
                        eng.wait_ge(r_ml, 2 * u + 2)
                        eng.wait_ge(r_oh, u + 1)
                        if u % GU == 0 and g >= 2:
                            eng.wait_ge(r_ad, g - 1)
                        ends = u % GU == GU - 1 or u == UNITS - 1
                        for j in range(4):
                            o = SG[g % 2][:, 0:D]
                            eng.matmul(o, oh[:, u % 2, j, :], mh[:, u % 2, j, :], start=(u % GU == 0 and j == 0), stop=False)
                            last = eng.matmul(o, oh[:, u % 2, j, :], ml[:, u % 2, j, :], start=False, stop=(ends and j == 3))
                        last.then_inc(r_sg, 1)

                    def window_turn(g):
                        eng.wait_ge(r_ev, g + 1)
                        for k in range(2):
                            last = eng.transpose(SG[g % 2][:, k * P:k * P + P], agw[:, g % 2, k * P:k * P + P], ident[:, :])
                        last.then_inc(r_tr, 1)

                    first_layer(0)
                    for u in range(UNITS):
                        if u + 1 < UNITS:
                            first_layer(u + 1)
                        second_layer(u)
                        if u >= 1:
                            segment(u - 1)
                        if u % GU == 1 and u >= GU:
                            window_turn(u // GU - 1)
                    if (UNITS - 1) % GU < 1:
                        window_turn(GROUPS - 2)
                    segment(UNITS - 1)
                    window_turn(GROUPS - 1)

        def general_path(tag):
            with ExitStack() as c:
                zz = sb(f"zz{tag}", [P, 2, D], F32, c)
                raw = sb(f"raw{tag}", [F, ST], F32, c)
                pl = sb(f"pol{tag}", [ST, 1], F32, c)
                gate = sb(f"gate{tag}", [ST, 1], F32, c)
                si = sb(f"si{tag}", [ST, 1], I32, c)
                di = sb(f"di{tag}", [ST, 1], I32, c)
                dbi = sb(f"dbi{tag}", [ST, ST], I32, c)
                df = sb(f"df{tag}", [ST, 1], F32, c)
                dbf = sb(f"dbf{tag}", [ST, ST], F32, c)
                eq = sb(f"eq{tag}", [ST, ST], F32, c)
                low = sb(f"low{tag}", [P, P], F32, c)
                lm = sb(f"lm{tag}", [ST, ST], F32, c)
                cnt = sb(f"cnt{tag}", [ST, 1], F32, c)
                dup = sb(f"dup{tag}", [ST, 1], F32, c)
                tr_i = sb(f"tr_i{tag}", [P, 1], I32, c)
                tr = sb(f"tr{tag}", [P, 1], F32, c)
                dl = sb(f"dl{tag}", [ST, 1], F32, c)
                tf = sb(f"tf{tag}", [ST, 1], F32, c)
                ti = sb(f"ti{tag}", [ST, 1], I32, c)
                hx = sb(f"hx{tag}", [ST, D], F32, c)
                hid = sb(f"hid{tag}", [P, 2, ST], F32, c)
                msg = sb(f"msg{tag}", [ST, D], F32, c)
                msr = sb(f"msr{tag}", [ST, D], F32, c)
                ssum = sb(f"ssum{tag}", [ST, D], F32, c)
                s0 = sem(f"s_g0{tag}", c)
                s1 = sem(f"s_g1{tag}", c)
                s2 = sem(f"s_g2{tag}", c)
                s3 = sem(f"s_g3{tag}", c)
                with nc.Block() as block:
                    @block.vector
                    def _(eng):
                        eng.memset(zz[:, :, :], 0.0).then_inc(s0, 1)
                        eng.wait_ge(s2, 1)
                        eng.tensor_copy(tr[:, :], tr_i[:, :])

                    @block.gpsimd
                    def _(eng):
                        eng.memset(low[:, :], 1.0).then_inc(s1, 1)
                        eng.iota(tr_i[:, :], pattern=[[0, 1]], base=NP, channel_multiplier=1).then_inc(s2, 1)
                        eng.wait_ge(s1, 1)
                        eng.affine_select(out=low[:, :], in_=low[:, :], compare_op=ALU.is_gt, fill=0.0,
                                          base=0, pattern=[[-1, P]], channel_multiplier=1)

                    @block.sync
                    def _(eng):
                        eng.wait_ge(s0, 1)
                        for t in range(0, NT + 1, 2):
                            eng.dma_start(aggd[t * P:(t + 2) * P, :].rearrange("(t p) d -> p t d", p=P),
                                          zz[:, :, :]).then_inc(s3, 16)
                        eng.wait_ge(s3, 16 * len(range(0, NT + 1, 2)))

                sl = sem(f"s_l{tag}", c)
                sg = sem(f"s_ga{tag}", c)
                s_l1 = sem(f"s_l1{tag}", c)
                s_hid = sem(f"s_hid{tag}", c)
                s_l2 = sem(f"s_l2{tag}", c)
                s_v = sem(f"s_v{tag}", c)
                s_ms = sem(f"s_ms{tag}", c)
                s_sum = sem(f"s_sum{tag}", c)
                s_ss = sem(f"s_ss{tag}", c)
                s_sc = sem(f"s_sc{tag}", c)
                every = [sl, s_l1, s_hid, s_l2, s_v, s_ms, s_sum, s_ss]
                with nc.Fori(0, NS) as i:
                    with nc.Block() as block:
                        @block.sync
                        def _(eng):
                            for s in every:
                                eng.sem_clear(s)

                        @block.gpsimd
                        def _(eng):
                            eng.dma_reset(range(sg.num, sg.num + 1))
                            eng.dma_reset(range(s_sc.num, s_sc.num + 1))
                            eng.sem_clear(sg)
                            eng.sem_clear(s_sc)

                    with nc.Block() as block:
                        @block.sync
                        def _(eng):
                            e0 = i * ST
                            eng.dma_start(raw[:, :], attrT[1:1 + F, bass.ds(e0, ST)]).then_inc(sl, 16)
                            eng.dma_start(pl[:, :], pol[bass.ds(e0, ST)][:, None]).then_inc(sl, 16)
                            eng.dma_start(si[:, :], src[bass.ds(e0, ST)][:, None]).then_inc(sl, 16)
                            eng.dma_start(di[:, :], dst[bass.ds(e0, ST)][:, None]).then_inc(sl, 16)
                            eng.dma_start(dbi[:, :], dst[bass.ds(e0, ST)][None, :].broadcast_to([ST, ST])).then_inc(sl, 16)

                        @block.gpsimd
                        def _(eng):
                            eng.wait_ge(sl, 80)
                            eng.indirect_dma_start(out=hx[:, :], out_offset=None, in_=tables,
                                                   in_offset=bass.IndirectOffsetOnAxis(ap=si[:, 0:1], axis=0)).then_inc(sg, 16)
                            eng.wait_ge(s_ss, 1)
                            eng.indirect_dma_start(out=aggd,
                                                   out_offset=bass.IndirectOffsetOnAxis(ap=ti[:, 0:1], axis=0),
                                                   in_=ssum[:, :], in_offset=None, compute_op=ALU.add).then_inc(s_sc, 16)
                            eng.wait_ge(s_sc, 16)

                        @block.tensor
                        def _(eng):
                            eng.wait_ge(sl, 80)
                            for k in range(2):
                                last = eng.matmul(bank[k][:, 0:ST], w1[0:F, k * P:k * P + P], raw[:, :], start=True, stop=True)
                            last.then_inc(s_l1, 1)
                            eng.wait_ge(s_hid, 1)
                            for k in range(2):
                                eng.matmul(bank[2][0:ST, 0:D], hid[:, k, :], wc[:, k, :], start=(k == 0), stop=False)
                            eng.matmul(bank[2][0:ST, 0:D], ones[0:1, 0:ST], c2[:, :], start=False, stop=True).then_inc(s_l2, 1)
                            eng.wait_ge(s_ms, 1)
                            eng.matmul(bank[3][0:ST, 0:D], eq[:, :], msr[:, :], start=True, stop=True).then_inc(s_sum, 1)

                        @block.scalar
                        def _(eng):
                            eng.wait_ge(s_l1, 1)
                            for k in range(2):
                                last = eng.activation(hid[:, k, :], bank[k][:, 0:ST], ACT.Relu, bias=b1[:, k:k + 1])
                            last.then_inc(s_hid, 1)

                        @block.vector
                        def _(eng):
                            n = [0]

                            def link(ins):
                                n[0] += 1
                                ins.then_inc(s_v, 1)
                                eng.wait_ge(s_v, n[0])

                            eng.wait_ge(sl, 80)
                            link(eng.tensor_scalar(gate[:, :], pl[:, :], 0.0, 1.0, ALU.max, ALU.min))
                            link(eng.tensor_scalar(gate[:, :], gate[:, :], 0.01, None, ALU.add))
                            link(eng.tensor_copy(df[:, :], di[:, :]))
                            link(eng.tensor_copy(dbf[:, :], dbi[:, :]))
                            link(eng.tensor_scalar(eq[:, :], dbf[:, :], df[:, 0:1], None, ALU.is_equal))
                            link(eng.tensor_tensor(lm[:, :], eq[:, :], low[0:ST, 0:ST], ALU.mult))
                            link(eng.tensor_reduce(cnt[:, :], lm[:, :], axis=AX.X, op=ALU.max))
                            link(eng.tensor_tensor(dl[:, :], tr[0:ST, :], df[:, :], ALU.subtract))
                            link(eng.tensor_tensor(dup[:, :], dl[:, :], cnt[:, :], ALU.mult))
                            link(eng.tensor_tensor(tf[:, :], dup[:, :], df[:, :], ALU.add))
                            link(eng.tensor_copy(ti[:, :], tf[:, :]))
                            eng.wait_ge(s_l2, 1)
                            eng.wait_ge(sg, 16)
                            link(eng.scalar_tensor_tensor(out=msg[:, :], in0=bank[2][0:ST, 0:D], scalar=gate[:, 0:1],
                                                          in1=hx[:, :], op0=ALU.mult, op1=ALU.add))
                            eng.tensor_scalar(msr[:, :], msg[:, :], 0.0, None, ALU.max).then_inc(s_ms, 1)
                            eng.wait_ge(s_sum, 1)
                            eng.tensor_copy(ssum[:, :], bank[3][0:ST, 0:D]).then_inc(s_ss, 1)

                ag = sb(f"ag{tag}", [P, 2, D], F32, c)
                s_al = [sem(f"s_al{tag}{i}", c) for i in range(2)]
                s_at = sem(f"s_at{tag}", c)
                s_ad = sem(f"s_ad{tag}", c)
                with nc.Block() as block:
                    @block.sync
                    def _(eng):
                        for t in range(NT):
                            if t >= 2:
                                eng.wait_ge(s_at, t - 1)
                            eng.dma_start(ag[:, t % 2, :], aggd[t * P:(t + 1) * P, :]).then_inc(s_al[t % 2], 16)

                    @block.tensor
                    def _(eng):
                        for t in range(NT):
                            eng.wait_ge(s_al[t % 2], 16 * (t // 2 + 1))
                            if t >= 2:
                                eng.wait_ge(s_ad, t - 1)
                            for k in range(2):
                                last = eng.transpose(bank[t % 2][:, k * P:k * P + P], ag[:, t % 2, k * P:k * P + P], ident[:, :])
                            last.then_inc(s_at, 1)

                    @block.vector
                    def _(eng):
                        for t in range(NT):
                            eng.wait_ge(s_at, t + 1)
                            to = aggT[:, :, t * P:(t + 1) * P]
                            eng.tensor_tensor(to, bank[t % 2][:, 0:2 * P].rearrange("p (k n) -> p k n", k=2), to,
                                              ALU.add).then_inc(s_ad, 1)

        def epilogue():
            with ExitStack() as c:
                x_sb = sb("x_sbe", [P, NT, D], F32, c)
                s_x = sem("e_x", c)
                s_z = sem("e_z", c)
                g1 = sb("g1", [P, NT, D], F32, c)
                rT = sb("rT", [P, 2, 2, 512], F32, c)
                s_g1 = sem("e_g1", c)
                s_st = sem("e_st", c)
                s_cp = sem("e_cp", c)
                s_ag = sem("e_ag", c)
                s_sq = sem("e_sq", c)
                s_rs = sem("e_rs", c)
                s_n = sem("e_n", c)
                s_t = sem("e_t", c)
                s_r = sem("e_r", c)
                s_g2 = sem("e_g2", c)
                s_y = sem("e_y", c)
                s_xb = sem("e_xb", c)
                s_o = [sem(f"e_o{i}", c) for i in range(2)]
                block = c.enter_context(nc.Block())

                @block.tensor
                def _(eng):
                    for t in range(NT):
                        if t >= 4:
                            eng.wait_ge(s_cp, t - 3)
                        o = bank[t % 4][:, 0:D]
                        for k in range(2):
                            eng.matmul(o, aggT[:, k, t * P:(t + 1) * P], wg1[:, k, :], start=(k == 0), stop=False)
                        eng.matmul(o, ones[0:1, :], bg1[:, :], start=False, stop=True).then_inc(s_g1, 1)

                    def down(g):
                        t, n = NODE_GROUPS[g]
                        eng.wait_ge(s_r, g + 1)
                        for j in range(n):
                            q = t + j
                            if q >= 4:
                                eng.wait_ge(s_y, q - 3)
                            for k in range(2):
                                last = eng.matmul(bank[4 + q % 4][:, 0:D], rT[:, g % 2, k, j * P:j * P + P],
                                                  wg2[:, k, :], start=(k == 0), stop=(k == 1))
                            last.then_inc(s_g2, 1)

                    eng.wait_ge(s_cp, NT)
                    for g, (t, n) in enumerate(NODE_GROUPS):
                        eng.wait_ge(s_n, g + 1)
                        if g >= 2:
                            eng.wait_ge(s_r, g - 1)
                        for j in range(n):
                            for k in range(2):
                                last = eng.transpose(bank[2 * (g % 2) + k][:, j * P:j * P + P],
                                                     g1[:, t + j, k * P:k * P + P], ident[:, :])
                        last.then_inc(s_t, 1)
                        if g >= 1:
                            down(g - 1)
                    down(len(NODE_GROUPS) - 1)

                @block.vector
                def _(eng):
                    for t in range(NT):
                        eng.wait_ge(s_cp, t + 1)
                        eng.bn_stats(st[:, t, :], g1[:, t, :]).then_inc(s_st, 1)
                    eng.wait_ge(s_st, NT)
                    for t in range(NT):
                        last = eng.bn_aggr(mv[:, t, :], st[:, t, :])
                    last.then_inc(s_ag, 1)
                    eng.wait_ge(s_ag, 1)
                    eng.tensor_scalar(rs[:, :], mv[:, :, 1], EPS, None, ALU.add).then_inc(s_ag, 1)
                    eng.wait_ge(s_sq, 1)
                    eng.reciprocal(rs[:, :], rs[:, :]).then_inc(s_rs, 1)
                    eng.wait_ge(s_rs, 1)

                    def finish(g):
                        t, n = NODE_GROUPS[g]
                        for j in range(n):
                            eng.wait_ge(s_xb, t + j + 1)
                            eng.wait_ge(s_g2, t + j + 1)
                            eng.tensor_tensor(x_sb[:, t + j, :], bank[4 + (t + j) % 4][:, 0:D], x_sb[:, t + j, :],
                                              ALU.add).then_inc(s_y, 1)

                    for g, (t, n) in enumerate(NODE_GROUPS):
                        for j in range(n):
                            last = eng.tensor_scalar(g1[:, t + j, :], g1[:, t + j, :], mv[:, t + j, 0:1],
                                                     rs[:, t + j:t + j + 1], ALU.subtract, ALU.mult)
                        last.then_inc(s_n, 1)
                        if g >= 2:
                            finish(g - 2)
                    finish(len(NODE_GROUPS) - 2)
                    finish(len(NODE_GROUPS) - 1)

                @block.gpsimd
                def _(eng):
                    eng.memset(x_sb[96:P, NT - 1, :], 0.0).then_inc(s_z, 1)
                    eng.wait_ge(s_x, 32)
                    for t in range(NT):
                        eng.tensor_tensor(x_sb[:, t, :], x_sb[:, t, :], bg2[:, :], ALU.add).then_inc(s_xb, 1)

                @block.scalar
                def _(eng):
                    for t in range(NT):
                        eng.wait_ge(s_g1, t + 1)
                        eng.copy(g1[:, t, :], bank[t % 4][:, 0:D]).then_inc(s_cp, 1)
                    eng.wait_ge(s_ag, 2)
                    eng.activation(rs[:, :], rs[:, :], ACT.Sqrt).then_inc(s_sq, 1)
                    for g, (t, n) in enumerate(NODE_GROUPS):
                        eng.wait_ge(s_t, g + 1)
                        if g >= 2:
                            tt, m = NODE_GROUPS[g - 2]
                            eng.wait_ge(s_g2, tt + m)
                        for k in range(2):
                            last = eng.activation(rT[:, g % 2, k, 0:n * P], bank[2 * (g % 2) + k][:, 0:n * P], ACT.Relu,
                                                  bias=lnb[:, k:k + 1], scale=lng[:, k:k + 1])
                        last.then_inc(s_r, 1)

                @block.sync
                def _(eng):
                    eng.dma_start(x_sb[:, 0:NT - 1, :],
                                  x[0:(NT - 1) * P, :].rearrange("(t p) d -> p t d", p=P)).then_inc(s_x, 16)
                    eng.wait_ge(s_z, 1)
                    eng.dma_start(x_sb[0:LAST, NT - 1, :], x[(NT - 1) * P:N, :]).then_inc(s_x, 16)
                    for g, (t, n) in enumerate(NODE_GROUPS):
                        eng.wait_ge(s_y, t + n)
                        if t + n < NT:
                            eng.dma_start(out[t * P:(t + n) * P, :].rearrange("(t p) d -> p t d", p=P),
                                          x_sb[:, t:t + n, :]).then_inc(s_o[g % 2], 16)
                        else:
                            eng.dma_start(out[t * P:N, :], x_sb[0:LAST, t, :]).then_inc(s_o[g % 2], 16)
                    for i in range(2):
                        eng.wait_ge(s_o[i], 16 * len(range(i, len(NODE_GROUPS), 2)))

        setup()
        node_prelude("a")
        edge_path()
        crowded = nc.values_load(flag_i[0:1, 0:1], min_val=0, max_val=P)
        with nc.If(crowded > 0):
            node_prelude("b")
            general_path("b")
        epilogue()


def kernel(**inputs):
    import numpy as _np
    import concourse.bacc as _bacc
    from concourse import mybir as _mybir
    from concourse.bass_utils import run_bass_kernel_spmd as _run

    w = {k: _np.asarray(v) for k, v in inputs.items()}
    p = "L0_gnn_"
    data = [
        ("x", w["x"]), ("src", w["src"]), ("dst", w["dst"]),
        ("src_m", w["src"][:FULL * P].reshape(FULL, P).T), ("dst_m", w["dst"][:FULL * P].reshape(FULL, P).T),
        ("pol_m", w["edge_attr_65"][:FULL * P, 0].reshape(FULL, P).T), ("pol", w["edge_attr_65"][:, 0]),
        ("first", w["dst"][::GE]),
        ("attrT", _np.ascontiguousarray(w["edge_attr_65"].T)),
        ("W_e1T", _np.ascontiguousarray(w[p + "W_e1"].T)), ("b_e1", w[p + "b_e1"].reshape(2, P).T), ("b_e1r", w[p + "b_e1"]),
        ("W_e2", w[p + "W_e2"]), ("b_e2", w[p + "b_e2"].reshape(2, P).T),
        ("W_leT", _np.ascontiguousarray(w[p + "W_le"].T)), ("b_le", w[p + "b_le"]),
        ("W_g1T", _np.ascontiguousarray(w[p + "W_g1"].T)), ("b_g1", w[p + "b_g1"]),
        ("ln_g", w[p + "ln_g"].reshape(2, P).T), ("ln_b", w[p + "ln_b"].reshape(2, P).T),
        ("W_g2T", _np.ascontiguousarray(w[p + "W_g2"].T)), ("b_g2", w[p + "b_g2"]),
    ]
    nc = _bacc.Bacc("TRN2", target_bir_lowering=False, num_devices=1)
    arrays, args = {}, []
    for name, a in data:
        a = _np.ascontiguousarray(a)
        arrays[f"in_{name}"] = a
        args.append(nc.dram_tensor(f"in_{name}", a.shape, _mybir.dt.from_np(a.dtype), kind="ExternalInput").ap())
    o = nc.dram_tensor("out_0", (N, D), _mybir.dt.float32, kind="ExternalOutput").ap()
    gnn(nc, *args, o)
    r = _run(nc, [arrays], core_ids=[0])
    return r.results[0]["out_0"]
```

```python
import concourse.bass as bass
from concourse import mybir
from contextlib import ExitStack

F32 = mybir.dt.float32
F32R = mybir.dt.float32r
I32 = mybir.dt.int32
ALU = mybir.AluOpType
ACT = mybir.ActivationFunctionType
AX = mybir.AxisListType

N = 6250
E = 206250
D = 256
F = 64
EPS = 1e-05
P = 128
NT = 49
NP = NT * P
LAST = N - (NT - 1) * P
ST = 125
NS = E // ST
TILES = (E + P - 1) // P
FULL = E // P
TAIL = E - FULL * P
UNITS = TILES // 4
GU = 7
GROUPS = (UNITS + GU - 1) // GU
GE = GU * 4 * P
TOP = NP - P
NR = 3
NX = 4
NM = 4
AHEAD = 5
FUSE = 8
SPLIT = 9
GATES = (4, 5, 7, 9)
OWN = 5
NODE_GROUPS = [(4 * g, min(4, NT - 4 * g)) for g in range((NT + 3) // 4)]


def gnn(nc, x, src, dst, src_m, dst_m, pol_m, pol, first, attrT, W_e1T, b_e1, b_e1r, W_e2, b_e2, W_leT, b_le,
        W_g1T, b_g1, ln_g, ln_b, W_g2T, b_g2, out):
    ctx = ExitStack()
    with ctx:
        tables = nc.dram_tensor("gather_table", [NP, D], F32, kind="Internal").ap()
        aggd = nc.dram_tensor("aggregate_table", [NP + P, D], F32, kind="Internal").ap()

        def sb(name, shape, dt=F32, c=ctx):
            return c.enter_context(nc.sbuf_tensor(name, shape, dt))

        def sem(name, c=ctx):
            return c.enter_context(nc.semaphore(name))

        bank = [ctx.enter_context(nc.psum_tensor(f"bank{i}", [P, 512], F32)) for i in range(8)]
        ident = sb("ident", [P, P])
        ones = sb("ones", [P, P])
        iota = sb("iota", [P, P])
        aggT = sb("aggT", [P, 2, NP])
        w1 = sb("w1", [P, D])
        w1r = sb("w1r", [P, 2, D], F32R)
        wcr = sb("wcr", [P, 2, 2, D], F32R)
        c2r = sb("c2r", [P, D], F32R)
        g1r = sb("g1r", [P, D], F32R)
        onr = sb("onr", [P, P], F32R)
        sidx = sb("sidx", [P, TILES], I32)
        slot = sb("slot", [P, TILES])
        gt = sb("gt", [P, TILES])
        base = sb("base", [P, GROUPS])
        base_i = sb("base_i", [1, GROUPS], I32)
        flag_i = sb("flag_i", [1, 1], I32)
        b1 = sb("b1", [P, 2])
        wc = sb("wc", [P, 2, D])
        c2 = sb("c2", [1, D])
        ble = sb("ble", [P, D])
        lng = sb("lng", [P, 2])
        lnb = sb("lnb", [P, 2])
        bg2 = sb("bg2", [P, D])
        wgr = sb("wgr", [P, 4, 2, D], F32R)
        st = sb("st", [P, NT, 6])
        mv = sb("mv", [P, NT, 2])
        rs = sb("rs", [P, NT])

        def setup(c):
            we2 = sb("we2", [P, 2, D], F32, c)
            wle = sb("wle", [P, 2, D], F32, c)
            wg1 = sb("wg1", [P, 2, D], F32, c)
            wg2 = sb("wg2", [P, 2, D], F32, c)
            btmp = sb("btmp", [P, D], F32, c)
            btmr = sb("btmr", [P, D], F32R, c)
            bg1 = sb("bg1", [1, D], F32, c)
            be2 = sb("be2", [P, 2], F32, c)
            iota_i = sb("iota_i", [P, P], I32, c)
            dst_i = sb("dst_i", [P, TILES], I32, c)
            first_i = sb("first_i", [P, GROUPS], I32, c)
            low2 = sb("low2", [P, 4], F32, c)
            bad = sb("bad", [P, 1], F32, c)
            s_w = sem("s_w", c)
            s_i = sem("s_i", c)
            s_g = sem("s_g", c)
            s_m = sem("s_m", c)
            s_io = sem("s_io", c)
            s_z = sem("s_zp", c)
            s_c = sem("s_c", c)
            s_v = sem("s_v", c)
            s_bad = sem("s_bad", c)
            s_f = sem("s_f", c)
            loads = [
                (w1[0:F, :], W_e1T), (w1[F:P, :], W_e1T),
                (btmp[64:65, :], b_e1r[None, :]), (btmp[96:97, :], b_e1r[None, :]),
                (b1[:, :], b_e1),
                (we2[:, :, :], W_e2.rearrange("(k p) n -> p k n", p=P)),
                (be2[:, :], b_e2),
                (wle[:, :, :], W_leT.rearrange("(k p) n -> p k n", p=P)),
                (wg1[:, :, :], W_g1T.rearrange("(k p) n -> p k n", p=P)),
                (bg1[:, :], b_g1[None, :]),
                (lng[:, :], ln_g),
                (lnb[:, :], ln_b),
                (wg2[:, :, :], W_g2T.rearrange("(k p) n -> p k n", p=P)),
                (bg2[:, :], b_g2[None, :].broadcast_to([P, D])),
            ]
            edges = [
                (dst_i[:, 0:FULL], dst_m), (dst_i[0:TAIL, FULL:TILES], dst[FULL * P:E][:, None]),
                (sidx[:, 0:FULL], src_m), (sidx[0:TAIL, FULL:TILES], src[FULL * P:E][:, None]),
                (gt[:, 0:FULL], pol_m), (gt[0:TAIL, FULL:TILES], pol[FULL * P:E][:, None]),
                (first_i[:, :], first[None, :].broadcast_to([P, GROUPS])),
            ]

            def weights(eng):
                for dst_ap, src_ap in loads:
                    eng.dma_start(dst_ap, src_ap).then_inc(s_w, 16)

            def indices(eng):
                eng.wait_ge(s_z, 3)
                for dst_ap, src_ap in edges:
                    eng.dma_start(dst_ap, src_ap).then_inc(s_i, 16)

            def gpsimd(eng):
                eng.memset(dst_i[:, FULL:TILES], 0).then_inc(s_z, 1)
                eng.memset(sidx[:, FULL:TILES], 0).then_inc(s_z, 1)
                eng.memset(gt[:, FULL:TILES], 0.0).then_inc(s_z, 1)
                eng.memset(ones[:, :], 1.0).then_inc(s_m, 1)
                eng.memset(onr[:, :].bitcast(F32), 1.0).then_inc(s_m, 1)
                eng.memset(c2r[:, :].bitcast(F32), 0.0).then_inc(s_m, 1)
                eng.memset(g1r[:, :].bitcast(F32), 0.0).then_inc(s_m, 1)
                eng.memset(w1r[:, 1, :].bitcast(F32), 0.0).then_inc(s_m, 1)
                eng.iota(iota_i[:, :], pattern=[[1, P]], base=0, channel_multiplier=0).then_inc(s_io, 1)
                eng.wait_ge(s_z, 3)
                eng.wait_ge(s_m, 5)
                eng.wait_ge(s_io, 1)
                eng.memset(m2[64:P, :, :].bitcast(F32), 0.0).then_inc(r_m2, 1)
                eng.wait_ge(r_m2, 1)
                eng.memset(m2[64:65, :, :].bitcast(F32), 1.0).then_inc(r_m2, 1)
                eng.wait_ge(r_m2, 2)
                eng.memset(m2[96:97, :, :].bitcast(F32), 1.0).then_inc(r_m2, 1)
                eng.wait_ge(r_m2, 3)

            def gates(eng):
                eng.wait_ge(s_i, 16 * len(edges))
                for i, (c0, c1) in enumerate([(0, TILES // 2), (TILES // 2, TILES)]):
                    eng.tensor_scalar(gt[:, c0:c1], gt[:, c0:c1], 0.0, 1.0, ALU.max, ALU.min).then_inc(s_g, 1)
                    yield
                    eng.wait_ge(s_g, i + 1)
                    eng.tensor_scalar(gt[:, c0:c1], gt[:, c0:c1], 0.01, None, ALU.add)
                    yield

            def fuse(eng):
                eng.wait_ge(s_w, 16 * len(loads))
                for k in range(2):
                    for m in range(2):
                        eng.matmul(bank[0][:, D * k:D * k + D], we2[:, m, P * k:P * k + P], wle[:, m, :],
                                   start=(m == 0), stop=(m == 1))
                for m in range(2):
                    last = eng.matmul(bank[1][0:1, 0:D], be2[:, m:m + 1], wle[:, m, :],
                                      start=(m == 0), stop=(m == 1))
                last.then_inc(s_c, 1)

            def count_bad(eng):
                eng.wait_ge(s_bad, 1)
                eng.wait_ge(s_m, 5)
                eng.matmul(bank[2][0:1, 0:1], bad[:, 0:1], ones[:, 0:1], start=True, stop=True).then_inc(s_f, 1)

            def vector(eng):
                n = [0]

                def link(ins):
                    n[0] += 1
                    ins.then_inc(s_v, 1)
                    eng.wait_ge(s_v, n[0])

                w = 4 * GU
                m = FULL // w
                sv = slot[:, 0:m * w].rearrange("p (g k) -> p g k", k=w)
                bv = base[:, 0:m].rearrange("p (g k) -> p g k", k=1).broadcast_to([P, m, w])
                eng.wait_ge(s_io, 1)
                eng.tensor_copy(iota[:, :], iota_i[:, :])
                eng.memset(low2[:, :], 0.0)
                yield
                eng.wait_ge(s_i, 16 * len(edges))
                eng.tensor_copy(base[:, :], first_i[:, :])
                link(eng.tensor_copy(slot[:, :], dst_i[:, :]))
                link(eng.tensor_scalar(base[:, :], base[:, :], float(TOP), None, ALU.min))
                yield
                eng.tensor_copy(base_i[:, :], base[0:1, :])
                eng.tensor_tensor(sv, bv, sv, ALU.subtract)
                link(eng.tensor_scalar(slot[:, m * w:TILES], slot[:, m * w:TILES], -1.0, base[:, m:m + 1],
                                       ALU.mult, ALU.add))
                yield
                eng.tensor_reduce(low2[:, 0:1], slot[:, 0:FULL], axis=AX.X, op=ALU.max)
                yield
                eng.tensor_reduce(low2[:, 1:2], slot[:, 0:FULL], axis=AX.X, op=ALU.min)
                yield
                eng.tensor_copy(low2[0:TAIL, 2:3], slot[0:TAIL, FULL:TILES])
                link(eng.tensor_copy(low2[0:TAIL, 3:4], slot[0:TAIL, FULL:TILES]))
                link(eng.tensor_scalar(low2[:, 0:4:2], low2[:, 0:4:2], 0.0, None, ALU.is_gt))
                link(eng.tensor_scalar(low2[:, 1:4:2], low2[:, 1:4:2], float(1 - P), None, ALU.is_lt))
                eng.tensor_reduce(bad[:, 0:1], low2[:, :], axis=AX.X, op=ALU.max).then_inc(s_bad, 1)
                yield
                eng.wait_ge(s_w, 16 * len(loads))
                eng.wait_ge(s_m, 5)
                eng.tensor_copy(g1r[0:1, :], bg1[:, :])
                eng.tensor_copy(wgr[:, 0, :, :], wg1[:, :, :])
                link(eng.tensor_copy(wgr[:, 2, :, :], wg2[:, :, :]))
                yield
                eng.tensor_tensor(g1r[32:33, :], bg1[:, :], g1r[0:1, :].bitcast(F32), ALU.subtract)
                eng.tensor_tensor(wgr[:, 1, :, :], wg1[:, :, :], wgr[:, 0, :, :].bitcast(F32), ALU.subtract)
                yield
                eng.tensor_tensor(wgr[:, 3, :, :], wg2[:, :, :], wgr[:, 2, :, :].bitcast(F32), ALU.subtract)
                eng.tensor_copy(w1r[:, 0, :], w1[:, :])
                link(eng.tensor_copy(btmr[64:65, :], btmp[64:65, :]))
                yield
                link(eng.tensor_copy(btmr[96:97, :], btmp[96:97, :]))
                eng.tensor_tensor(w1r[0:F, 1, :], w1[0:F, :], w1r[0:F, 0, :].bitcast(F32), ALU.subtract)
                eng.tensor_copy(w1r[64:65, 1, :], btmp[64:65, :])
                eng.tensor_tensor(w1r[96:97, 1, :], btmp[96:97, :], btmr[96:97, :].bitcast(F32), ALU.subtract)
                yield
                eng.wait_ge(s_c, 1)
                link(eng.tensor_copy(wc[:, :, :], bank[0][:, :].rearrange("p (k n) -> p k n", k=2)))
                link(eng.tensor_copy(c2[:, :], bank[1][0:1, 0:D]))
                yield
                eng.tensor_copy(c2r[0:1, :], c2[:, :])
                link(eng.tensor_copy(wcr[:, 0, :, :], wc[:, :, :]))
                eng.tensor_tensor(c2r[32:33, :], c2[:, :], c2r[0:1, :].bitcast(F32), ALU.subtract)
                eng.tensor_tensor(wcr[:, 1, :, :], wc[:, :, :], wcr[:, 0, :, :].bitcast(F32), ALU.subtract)
                yield
                eng.wait_ge(s_f, 1)
                eng.tensor_copy(flag_i[:, :], bank[2][0:1, 0:1])
                yield

            return {"weights": weights, "indices": indices, "gpsimd": gpsimd, "gates": gates, "fuse": fuse, "count_bad": count_bad,
                    "vector": vector}

        def nodes(c, tag, s_o):
            x_sb = sb(f"x_sb{tag}", [P, NT, D], F32, c)
            h = sb(f"h{tag}", [P, 2, 4, D], F32, c)
            nb = sb(f"nb{tag}", [P, NT], F32, c)
            G = len(NODE_GROUPS)
            s_z = sem(f"s_z{tag}", c)
            s_bl = sem(f"s_bl{tag}", c)
            s_x = [sem(f"s_x{tag}_{i}", c) for i in range(G)]
            s_st = sem(f"s_st{tag}", c)
            s_ag = sem(f"s_ag{tag}", c)
            s_ep = sem(f"s_ep{tag}", c)
            s_sq = sem(f"s_sq{tag}", c)
            s_rs = sem(f"s_rs{tag}", c)
            s_n = sem(f"s_n{tag}", c)
            s_h = sem(f"s_h{tag}", c)
            s_hb = sem(f"s_hb{tag}", c)
            s_t = sem(f"s_t{tag}", c)
            s_e = sem(f"s_e{tag}", c)
            s_id = sem(f"s_id{tag}", c)

            def loads(eng, between=None):
                for g, (t, n) in enumerate(NODE_GROUPS[:-1]):
                    eng.dma_start(x_sb[:, t:t + n, :],
                                  x[t * P:(t + n) * P, :].rearrange("(t p) d -> p t d", p=P)).then_inc(s_x[g], 16)
                    if g == 0:
                        eng.dma_start(ble[:, :], b_le[None, :].broadcast_to([P, D])).then_inc(s_bl, 16)
                    if g == AHEAD and between is not None:
                        between(eng)
                eng.wait_ge(s_z, 1)
                eng.dma_start(x_sb[0:LAST, NT - 1, :], x[(NT - 1) * P:N, :]).then_inc(s_x[-1], 16)

            def stores(eng):
                for g, (t, n) in enumerate(NODE_GROUPS):
                    eng.wait_ge(s_hb, g + 1)
                    eng.dma_start(tables[t * P:(t + n) * P, :].rearrange("(t p) d -> p t d", p=P),
                                  x_sb[:, t:t + n, :]).then_inc(s_o, 16)
                    yield g

            def vector(eng):
                eng.memset(x_sb[96:P, NT - 1, :], 0.0).then_inc(s_z, 1)
                for s in range(G + 1):
                    if s < G:
                        t, n = NODE_GROUPS[s]
                        eng.wait_ge(s_x[s], 16)
                        for k in range(t, t + n):
                            last = eng.bn_stats(st[:, k, :], x_sb[:, k, :])
                        last.then_inc(s_st, 1)
                        eng.wait_ge(s_st, s + 1)
                        for k in range(t, t + n):
                            last = eng.bn_aggr(mv[:, k, :], st[:, k, :])
                        last.then_inc(s_ag, 1)
                        eng.wait_ge(s_ag, s + 1)
                        eng.tensor_scalar(rs[:, t:t + n], mv[:, t:t + n, 1], EPS, None, ALU.add).then_inc(s_ep, 1)
                    if s >= 1:
                        t, n = NODE_GROUPS[s - 1]
                        eng.wait_ge(s_sq, s)
                        eng.reciprocal(rs[:, t:t + n], rs[:, t:t + n]).then_inc(s_rs, 1)
                        eng.wait_ge(s_rs, s)
                        eng.scalar_tensor_tensor(out=nb[:, t:t + n], in0=mv[:, t:t + n, 0], scalar=-1.0,
                                                 in1=rs[:, t:t + n], op0=ALU.mult, op1=ALU.mult).then_inc(s_n, 1)
                    yield s

            def scalar(eng):
                def evacuate(g):
                    t, n = NODE_GROUPS[g]
                    eng.wait_ge(s_t, g + 1)
                    for k in range(2):
                        last = eng.copy(aggT[:, k, t * P:(t + n) * P], bank[4 + 2 * (g % 2) + k][:, 0:n * P])
                    last.then_inc(s_e, 1)

                def root(g):
                    t, n = NODE_GROUPS[g]
                    eng.wait_ge(s_ep, g + 1)
                    eng.activation(rs[:, t:t + n], rs[:, t:t + n], ACT.Sqrt).then_inc(s_sq, 1)

                root(0)
                for g, (t, n) in enumerate(NODE_GROUPS):
                    if g + 1 < G:
                        root(g + 1)
                    eng.wait_ge(s_n, g + 1)
                    if g >= 2:
                        eng.wait_ge(s_hb, g - 1)
                        eng.wait_ge(s_t, g - 1)
                    for j in range(n):
                        last = eng.activation(h[:, g % 2, j, :], x_sb[:, t + j, :], ACT.Relu,
                                              bias=nb[:, t + j:t + j + 1], scale=rs[:, t + j:t + j + 1])
                    last.then_inc(s_h, 1)
                    if g >= 1:
                        evacuate(g - 1)
                    yield g
                evacuate(G - 1)

            def gpsimd(eng):
                eng.memset(ident[:, :], 0.0).then_inc(s_id, 1)
                eng.wait_ge(s_id, 1)
                eng.affine_select(out=ident[:, :], in_=ident[:, :], compare_op=ALU.not_equal, fill=1.0,
                                  base=0, pattern=[[-1, P]], channel_multiplier=1).then_inc(s_id, 1)
                eng.wait_ge(s_bl, 16)
                for g, (t, n) in enumerate(NODE_GROUPS):
                    eng.wait_ge(s_h, g + 1)
                    eng.tensor_tensor(x_sb[:, t:t + n, :], h[:, g % 2, 0:n, :],
                                      ble[:, :].rearrange("p (a d) -> p a d", a=1).broadcast_to([P, n, D]),
                                      ALU.add).then_inc(s_hb, 1)
                    yield g

            def tensor(eng):
                eng.wait_ge(s_id, 2)
                for g, (t, n) in enumerate(NODE_GROUPS):
                    eng.wait_ge(s_h, g + 1)
                    if g >= 2:
                        eng.wait_ge(s_e, g - 1)
                    for j in range(n):
                        for k in range(2):
                            last = eng.transpose(bank[4 + 2 * (g % 2) + k][:, j * P:j * P + P],
                                                 h[:, g % 2, j, k * P:k * P + P], ident[:, :])
                    last.then_inc(s_t, 1)
                    yield g

            return {"loads": loads, "stores": stores, "vector": vector, "scalar": scalar, "gpsimd": gpsimd,
                    "tensor": tensor}

        s_oa = sem("s_oa")
        r_load = [sem(f"r_load{i}") for i in range(NR)]
        r_m2 = sem("r_m2")
        r_rh = sem("r_rh")
        r_rl = sem("r_rl")
        r_cp = [sem(f"r_cp{i}") for i in range(NM)]
        r_l1 = sem("r_l1")
        early = ExitStack()
        raw = sb("raw", [F, NR, 1024], F32, early)
        m1 = sb("m1", [P, NM, 512], F32R, early)
        m2 = sb("m2", [P, NM, 512], F32R, early)

        def part(u):
            return raw[:, (u // 2) % NR, 512 * (u % 2):512 * (u % 2) + 512]

        def loaded(eng, u):
            eng.wait_ge(r_load[(u // 2) % NR], 16 * ((u // 2) // NR + 1))

        def load_raw(eng, n):
            w = min(1024, E - 1024 * n)
            eng.dma_start(raw[:, n % NR, 0:w], attrT[1:1 + F, 1024 * n:1024 * n + w]).then_inc(r_load[n % NR], 16)

        def raw_high(eng, u):
            loaded(eng, u)
            if u >= NM:
                eng.wait_ge(r_l1, 2 * (u - NM) + 2)
            eng.copy(m1[0:F, u % NM, :], part(u)).then_inc(r_rh, 1)

        def raw_low(eng, u):
            loaded(eng, u)
            eng.wait_ge(r_rh, u + 1)
            eng.tensor_tensor(m1[F:P, u % NM, :], part(u), m1[0:F, u % NM, :].bitcast(F32),
                              ALU.subtract).then_inc(r_rl, 1)

        def second(eng, u):
            eng.wait_ge(r_rh, u + 1)
            eng.dma_start(m2[0:F, u % NM, :].bitcast(F32), m1[0:F, u % NM, :].bitcast(F32)).then_inc(r_cp[u % NM], 16)

        def prepare():
            with ExitStack() as c:
                b = nodes(c, "a", s_oa)
                a = setup(c)
                block = c.enter_context(nc.Block())

                @block.sync
                def _(eng):
                    b["loads"](eng, a["indices"])
                    a["weights"](eng)
                    for n in range(NR):
                        load_raw(eng, n)
                    for g in b["stores"](eng):
                        if g == SPLIT:
                            for u in range(3):
                                second(eng, u)

                @block.scalar
                def _(eng):
                    for g in b["scalar"](eng):
                        if g == SPLIT:
                            for u in range(3):
                                raw_high(eng, u)

                @block.gpsimd
                def _(eng):
                    a["gpsimd"](eng)
                    gates = a["gates"](eng)
                    for g in b["gpsimd"](eng):
                        if g in GATES:
                            next(gates, None)
                    for _ in gates:
                        pass

                @block.tensor
                def _(eng):
                    for g in b["tensor"](eng):
                        if g == FUSE:
                            a["fuse"](eng)
                    a["count_bad"](eng)

                @block.vector
                def _(eng):
                    own = a["vector"](eng)
                    for step in b["vector"](eng):
                        if step >= OWN:
                            next(own, None)
                    for _ in own:
                        pass
                    for u in range(3):
                        raw_low(eng, u)

        def nodes_again():
            with ExitStack() as c:
                s_ob = sem("s_ob", c)
                b = nodes(c, "b", s_ob)
                block = c.enter_context(nc.Block())

                @block.sync
                def _(eng):
                    b["loads"](eng)
                    for _ in b["stores"](eng):
                        pass
                    eng.wait_ge(s_ob, 16 * len(NODE_GROUPS))

                @block.scalar
                def _(eng):
                    for _ in b["scalar"](eng):
                        pass

                @block.gpsimd
                def _(eng):
                    for _ in b["gpsimd"](eng):
                        pass

                @block.tensor
                def _(eng):
                    for _ in b["tensor"](eng):
                        pass

                @block.vector
                def _(eng):
                    for _ in b["vector"](eng):
                        pass

        def edge_path():
            with ExitStack() as c:
                hx = sb("hx", [P, NX, 4, D], F32, c)
                mhl = sb("mhl", [P, 2, 4, 2, D], F32R, c)
                mh = mhl[:, :, :, 0, :]
                ml = mhl[:, :, :, 1, :]
                agw = sb("agw", [P, 2, D], F32, c)
                sb("still_stored", [P, NT * D - (NX * 4 + 2 * 4 + 2 * 4 + 2) * D], F32, c)
                hh = sb("hh", [P, 2, 2, 512], F32R, c)
                hl = sb("hl", [P, 2, 2, 512], F32R, c)
                oh = sb("oh", [P, 3, 4, P], F32R, c)
                away = sb("away", [P, 2, 4, P], F32, c)
                r_hx = [sem(f"r_hx{i}", c) for i in range(NX)]
                r_hh = sem("r_hh", c)
                r_hl = sem("r_hl", c)
                r_l2 = sem("r_l2", c)
                r_t = sem("r_t", c)
                r_mh = sem("r_mh", c)
                r_ml = sem("r_ml", c)
                r_oh = sem("r_oh", c)
                r_aw = sem("r_aw", c)
                r_sg = sem("r_sg", c)
                r_ev = sem("r_ev", c)
                r_su = sem("r_su", c)
                r_tr = sem("r_tr", c)
                r_ad = sem("r_ad", c)
                LA = [bank[0], bank[1]]
                LB = [bank[2], bank[3], bank[4], bank[5]]
                SG = [bank[6], bank[7]]
                block = c.enter_context(nc.Block())

                @block.sync
                def _(eng):
                    for n in range(NR, (UNITS + 1) // 2):
                        for u in range(max(3, 2 * (n - NR)), 2 * (n - NR) + 2):
                            second(eng, u)
                        eng.wait_ge(r_rl, 2 * (n - NR) + 2)
                        load_raw(eng, n)
                    for u in range(2 * ((UNITS + 1) // 2 - NR), UNITS):
                        second(eng, u)

                @block.gpsimd
                def _(eng):
                    eng.wait_ge(s_oa, 16 * len(NODE_GROUPS))
                    for u in range(UNITS):
                        if u >= NX:
                            eng.wait_ge(r_t, 2 * (u - NX) + 2)
                        for j in range(4):
                            t = 4 * u + j
                            eng.indirect_dma_start(out=hx[:, u % NX, j, :], out_offset=None, in_=tables,
                                                   in_offset=bass.IndirectOffsetOnAxis(ap=sidx[:, t:t + 1], axis=0)
                                                   ).then_inc(r_hx[u % NX], 16)

                @block.scalar
                def _(eng):
                    def hidden_high(u):
                        if u >= 2:
                            eng.wait_ge(r_l2, 2 * (u - 2) + 2)
                        for k in range(2):
                            eng.wait_ge(r_l1, 2 * u + k + 1)
                            eng.activation(hh[:, u % 2, k, :], LA[k][:, :], ACT.Relu).then_inc(r_hh, 1)

                    def message_high(u, q):
                        if u >= 2:
                            eng.wait_ge(r_sg, u - 1)
                        eng.wait_ge(r_t, 2 * u + q + 1)
                        eng.activation(mh[:, u % 2, 2 * q:2 * q + 2, :],
                                       LB[(2 * u + q) % 4][:, :].rearrange("p (j n) -> p j n", j=2),
                                       ACT.Relu).then_inc(r_mh, 1)

                    def onehot(u):
                        if u >= 2:
                            eng.wait_ge(r_oh, u - 1)
                        for j in range(4):
                            t = 4 * u + j
                            last = eng.activation(away[:, u % 2, j, :], iota[:, :], ACT.Abs, bias=slot[:, t:t + 1])
                        last.then_inc(r_aw, 1)

                    def onehot_end(u):
                        eng.wait_ge(r_aw, u + 1)
                        if u >= 3:
                            eng.wait_ge(r_sg, u - 2)
                        eng.activation(oh[:, u % 3, :, :], away[:, u % 2, :, :], ACT.Relu, bias=1.0,
                                       scale=-1.0).then_inc(r_oh, 1)

                    def window_out(g):
                        eng.wait_ge(r_sg, min(GU * g + GU, UNITS))
                        if g >= 2:
                            eng.wait_ge(r_tr, g - 1)
                        eng.copy(agw[:, g % 2, :], SG[g % 2][:, 0:D]).then_inc(r_ev, 1)

                    hidden_high(0)
                    onehot(0)
                    onehot_end(0)
                    for u in range(UNITS):
                        if u + 1 < UNITS:
                            hidden_high(u + 1)
                        if u >= 1:
                            onehot_end(u)
                        if u + 3 < UNITS:
                            raw_high(eng, u + 3)
                        if u + 1 < UNITS:
                            onehot(u + 1)
                        message_high(u, 0)
                        message_high(u, 1)
                        if u % GU == 0 and u >= GU:
                            window_out(u // GU - 1)
                    window_out(GROUPS - 1)

                @block.vector
                def _(eng):
                    def hidden_low(u):
                        if u >= 2:
                            eng.wait_ge(r_l2, 2 * (u - 2) + 2)
                        for k in range(2):
                            eng.wait_ge(r_hh, 2 * u + k + 1)
                            eng.scalar_tensor_tensor(out=hl[:, u % 2, k, :], in0=LA[k][:, :], scalar=0.0,
                                                     in1=hh[:, u % 2, k, :].bitcast(F32),
                                                     op0=ALU.max, op1=ALU.subtract).then_inc(r_hl, 1)

                    def total(u):
                        eng.wait_ge(r_hx[u % NX], 64 * (u // NX + 1))
                        for q in range(2):
                            eng.wait_ge(r_l2, 2 * u + q + 1)
                            for j in range(2):
                                t = 4 * u + 2 * q + j
                                b = LB[(2 * u + q) % 4][:, D * j:D * j + D]
                                last = eng.scalar_tensor_tensor(out=b, in0=b, scalar=gt[:, t:t + 1],
                                                                in1=hx[:, u % NX, 2 * q + j, :],
                                                                op0=ALU.mult, op1=ALU.add)
                            last.then_inc(r_t, 1)

                    def message_low(u):
                        if u >= 2:
                            eng.wait_ge(r_sg, u - 1)
                        for q in range(2):
                            eng.wait_ge(r_mh, 2 * u + q + 1)
                            eng.scalar_tensor_tensor(out=ml[:, u % 2, 2 * q:2 * q + 2, :],
                                                     in0=LB[(2 * u + q) % 4][:, :].rearrange("p (j n) -> p j n", j=2),
                                                     scalar=0.0,
                                                     in1=mh[:, u % 2, 2 * q:2 * q + 2, :].bitcast(F32),
                                                     op0=ALU.max, op1=ALU.subtract).then_inc(r_ml, 1)

                    def window_sum(g):
                        eng.wait_ge(r_ev, g + 1)
                        eng.tensor_tensor(agw[:, g % 2, :], agw[:, g % 2, :], SG[g % 2][:, D:2 * D],
                                          ALU.add).then_inc(r_su, 1)

                    def window_add(g):
                        b0 = eng.value_load(base_i[0:1, g:g + 1], min_val=0, max_val=TOP)
                        eng.wait_ge(r_tr, g + 1)
                        if g >= 1:
                            eng.wait_ge(r_ad, g)
                        to = aggT[:, :, bass.ds(b0, P)]
                        eng.tensor_tensor(to, to, SG[g % 2][:, 0:2 * P].rearrange("p (k n) -> p k n", k=2),
                                          ALU.add).then_inc(r_ad, 1)

                    hidden_low(0)
                    for u in range(UNITS):
                        if u + 1 < UNITS:
                            hidden_low(u + 1)
                        if u % GU == 1 and u >= GU:
                            window_sum(u // GU - 1)
                        total(u)
                        if u + 3 < UNITS:
                            raw_low(eng, u + 3)
                        message_low(u)
                        if u % GU == 2 and u >= GU:
                            window_add(u // GU - 1)
                    if (UNITS - 1) % GU < 1:
                        window_sum(GROUPS - 2)
                    if (UNITS - 1) % GU < 2:
                        window_add(GROUPS - 2)
                    window_sum(GROUPS - 1)
                    window_add(GROUPS - 1)

                @block.tensor
                def _(eng):
                    c2w = c2r[:, :].rearrange("p (a n) -> p a n", a=1).broadcast_to([P, 2, D])

                    def first_layer(u):
                        eng.wait_ge(r_rl, u + 1)
                        eng.wait_ge(r_cp[u % NM], 16 * (u // NM + 1))
                        if u == 0:
                            eng.wait_ge(r_m2, 3)
                        for k in range(2):
                            if u >= 1:
                                eng.wait_ge(r_hl, 2 * (u - 1) + k + 1)
                            eng.matmul(LA[k][:, :], w1r[:, 0, k * P:k * P + P], m1[:, u % NM, :], start=True, stop=False)
                            eng.matmul(LA[k][:, :], w1r[:, 1, k * P:k * P + P], m2[:, u % NM, :],
                                       start=False, stop=True).then_inc(r_l1, 1)

                    def second_layer(u):
                        eng.wait_ge(r_hh, 2 * u + 2)
                        eng.wait_ge(r_hl, 2 * u + 2)
                        for q in range(2):
                            if u >= 2:
                                eng.wait_ge(r_ml, 2 * (u - 2) + q + 1)
                            eng.matmul(LB[(2 * u + q) % 4][:, :], onr[:, :], c2w, start=True, stop=False)
                            for j in range(2):
                                o = LB[(2 * u + q) % 4][:, D * j:D * j + D]
                                e0 = (2 * q + j) * P
                                for k in range(2):
                                    eng.matmul(o, hh[:, u % 2, k, e0:e0 + P], wcr[:, 0, k, :], start=False, stop=False)
                                    eng.matmul(o, hh[:, u % 2, k, e0:e0 + P], wcr[:, 1, k, :], start=False, stop=False)
                                    last = eng.matmul(o, hl[:, u % 2, k, e0:e0 + P], wcr[:, 0, k, :],
                                                      start=False, stop=(j == 1 and k == 1))
                            last.then_inc(r_l2, 1)

                    def segment(u):
                        g = u // GU
                        eng.wait_ge(r_ml, 2 * u + 2)
                        eng.wait_ge(r_oh, u + 1)
                        if u % GU == 0 and g >= 2:
                            eng.wait_ge(r_ad, g - 1)
                        ends = u % GU == GU - 1 or u == UNITS - 1
                        for j in range(4):
                            last = eng.matmul(SG[g % 2][:, :], oh[:, u % 3, j, :], mhl[:, u % 2, j, :, :],
                                              start=(u % GU == 0 and j == 0), stop=(ends and j == 3))
                        last.then_inc(r_sg, 1)

                    def window_turn(g):
                        eng.wait_ge(r_su, g + 1)
                        for k in range(2):
                            last = eng.transpose(SG[g % 2][:, k * P:k * P + P], agw[:, g % 2, k * P:k * P + P], ident[:, :])
                        last.then_inc(r_tr, 1)

                    first_layer(0)
                    for u in range(UNITS):
                        if u + 1 < UNITS:
                            first_layer(u + 1)
                        second_layer(u)
                        if u >= 1:
                            segment(u - 1)
                        if u % GU == 1 and u >= GU:
                            window_turn(u // GU - 1)
                    if (UNITS - 1) % GU < 1:
                        window_turn(GROUPS - 2)
                    segment(UNITS - 1)
                    window_turn(GROUPS - 1)

        def general_path(tag):
            with ExitStack() as c:
                zz = sb(f"zz{tag}", [P, 2, D], F32, c)
                raw = sb(f"raw{tag}", [F, ST], F32, c)
                pl = sb(f"pol{tag}", [ST, 1], F32, c)
                gate = sb(f"gate{tag}", [ST, 1], F32, c)
                si = sb(f"si{tag}", [ST, 1], I32, c)
                di = sb(f"di{tag}", [ST, 1], I32, c)
                dbi = sb(f"dbi{tag}", [ST, ST], I32, c)
                df = sb(f"df{tag}", [ST, 1], F32, c)
                dbf = sb(f"dbf{tag}", [ST, ST], F32, c)
                eq = sb(f"eq{tag}", [ST, ST], F32, c)
                low = sb(f"low{tag}", [P, P], F32, c)
                lm = sb(f"lm{tag}", [ST, ST], F32, c)
                cnt = sb(f"cnt{tag}", [ST, 1], F32, c)
                dup = sb(f"dup{tag}", [ST, 1], F32, c)
                tr_i = sb(f"tr_i{tag}", [P, 1], I32, c)
                tr = sb(f"tr{tag}", [P, 1], F32, c)
                dl = sb(f"dl{tag}", [ST, 1], F32, c)
                tf = sb(f"tf{tag}", [ST, 1], F32, c)
                ti = sb(f"ti{tag}", [ST, 1], I32, c)
                hx = sb(f"hx{tag}", [ST, D], F32, c)
                hid = sb(f"hid{tag}", [P, 2, ST], F32, c)
                msg = sb(f"msg{tag}", [ST, D], F32, c)
                msr = sb(f"msr{tag}", [ST, D], F32, c)
                ssum = sb(f"ssum{tag}", [ST, D], F32, c)
                s0 = sem(f"s_g0{tag}", c)
                s1 = sem(f"s_g1{tag}", c)
                s2 = sem(f"s_g2{tag}", c)
                s3 = sem(f"s_g3{tag}", c)
                with nc.Block() as block:
                    @block.vector
                    def _(eng):
                        eng.memset(zz[:, :, :], 0.0).then_inc(s0, 1)
                        eng.wait_ge(s2, 1)
                        eng.tensor_copy(tr[:, :], tr_i[:, :])

                    @block.gpsimd
                    def _(eng):
                        eng.memset(low[:, :], 1.0).then_inc(s1, 1)
                        eng.iota(tr_i[:, :], pattern=[[0, 1]], base=NP, channel_multiplier=1).then_inc(s2, 1)
                        eng.wait_ge(s1, 1)
                        eng.affine_select(out=low[:, :], in_=low[:, :], compare_op=ALU.is_gt, fill=0.0,
                                          base=0, pattern=[[-1, P]], channel_multiplier=1)

                    @block.sync
                    def _(eng):
                        eng.wait_ge(s0, 1)
                        for t in range(0, NT + 1, 2):
                            eng.dma_start(aggd[t * P:(t + 2) * P, :].rearrange("(t p) d -> p t d", p=P),
                                          zz[:, :, :]).then_inc(s3, 16)
                        eng.wait_ge(s3, 16 * len(range(0, NT + 1, 2)))

                sl = sem(f"s_l{tag}", c)
                sg = sem(f"s_ga{tag}", c)
                s_l1 = sem(f"s_l1{tag}", c)
                s_hid = sem(f"s_hid{tag}", c)
                s_l2 = sem(f"s_l2{tag}", c)
                s_v = sem(f"s_v{tag}", c)
                s_ms = sem(f"s_ms{tag}", c)
                s_sum = sem(f"s_sum{tag}", c)
                s_ss = sem(f"s_ss{tag}", c)
                s_sc = sem(f"s_sc{tag}", c)
                every = [sl, s_l1, s_hid, s_l2, s_v, s_ms, s_sum, s_ss]
                with nc.Fori(0, NS) as i:
                    with nc.Block() as block:
                        @block.sync
                        def _(eng):
                            for s in every:
                                eng.sem_clear(s)

                        @block.gpsimd
                        def _(eng):
                            eng.dma_reset(range(sg.num, sg.num + 1))
                            eng.dma_reset(range(s_sc.num, s_sc.num + 1))
                            eng.sem_clear(sg)
                            eng.sem_clear(s_sc)

                    with nc.Block() as block:
                        @block.sync
                        def _(eng):
                            e0 = i * ST
                            eng.dma_start(raw[:, :], attrT[1:1 + F, bass.ds(e0, ST)]).then_inc(sl, 16)
                            eng.dma_start(pl[:, :], pol[bass.ds(e0, ST)][:, None]).then_inc(sl, 16)
                            eng.dma_start(si[:, :], src[bass.ds(e0, ST)][:, None]).then_inc(sl, 16)
                            eng.dma_start(di[:, :], dst[bass.ds(e0, ST)][:, None]).then_inc(sl, 16)
                            eng.dma_start(dbi[:, :], dst[bass.ds(e0, ST)][None, :].broadcast_to([ST, ST])).then_inc(sl, 16)

                        @block.gpsimd
                        def _(eng):
                            eng.wait_ge(sl, 80)
                            eng.indirect_dma_start(out=hx[:, :], out_offset=None, in_=tables,
                                                   in_offset=bass.IndirectOffsetOnAxis(ap=si[:, 0:1], axis=0)).then_inc(sg, 16)
                            eng.wait_ge(s_ss, 1)
                            eng.indirect_dma_start(out=aggd,
                                                   out_offset=bass.IndirectOffsetOnAxis(ap=ti[:, 0:1], axis=0),
                                                   in_=ssum[:, :], in_offset=None, compute_op=ALU.add).then_inc(s_sc, 16)
                            eng.wait_ge(s_sc, 16)

                        @block.tensor
                        def _(eng):
                            eng.wait_ge(sl, 80)
                            for k in range(2):
                                last = eng.matmul(bank[k][:, 0:ST], w1[0:F, k * P:k * P + P], raw[:, :], start=True, stop=True)
                            last.then_inc(s_l1, 1)
                            eng.wait_ge(s_hid, 1)
                            for k in range(2):
                                eng.matmul(bank[2][0:ST, 0:D], hid[:, k, :], wc[:, k, :], start=(k == 0), stop=False)
                            eng.matmul(bank[2][0:ST, 0:D], ones[0:1, 0:ST], c2[:, :], start=False, stop=True).then_inc(s_l2, 1)
                            eng.wait_ge(s_ms, 1)
                            eng.matmul(bank[3][0:ST, 0:D], eq[:, :], msr[:, :], start=True, stop=True).then_inc(s_sum, 1)

                        @block.scalar
                        def _(eng):
                            eng.wait_ge(s_l1, 1)
                            for k in range(2):
                                last = eng.activation(hid[:, k, :], bank[k][:, 0:ST], ACT.Relu, bias=b1[:, k:k + 1])
                            last.then_inc(s_hid, 1)

                        @block.vector
                        def _(eng):
                            n = [0]

                            def link(ins):
                                n[0] += 1
                                ins.then_inc(s_v, 1)
                                eng.wait_ge(s_v, n[0])

                            eng.wait_ge(sl, 80)
                            link(eng.tensor_scalar(gate[:, :], pl[:, :], 0.0, 1.0, ALU.max, ALU.min))
                            link(eng.tensor_scalar(gate[:, :], gate[:, :], 0.01, None, ALU.add))
                            link(eng.tensor_copy(df[:, :], di[:, :]))
                            link(eng.tensor_copy(dbf[:, :], dbi[:, :]))
                            link(eng.tensor_scalar(eq[:, :], dbf[:, :], df[:, 0:1], None, ALU.is_equal))
                            link(eng.tensor_tensor(lm[:, :], eq[:, :], low[0:ST, 0:ST], ALU.mult))
                            link(eng.tensor_reduce(cnt[:, :], lm[:, :], axis=AX.X, op=ALU.max))
                            link(eng.tensor_tensor(dl[:, :], tr[0:ST, :], df[:, :], ALU.subtract))
                            link(eng.tensor_tensor(dup[:, :], dl[:, :], cnt[:, :], ALU.mult))
                            link(eng.tensor_tensor(tf[:, :], dup[:, :], df[:, :], ALU.add))
                            link(eng.tensor_copy(ti[:, :], tf[:, :]))
                            eng.wait_ge(s_l2, 1)
                            eng.wait_ge(sg, 16)
                            link(eng.scalar_tensor_tensor(out=msg[:, :], in0=bank[2][0:ST, 0:D], scalar=gate[:, 0:1],
                                                          in1=hx[:, :], op0=ALU.mult, op1=ALU.add))
                            eng.tensor_scalar(msr[:, :], msg[:, :], 0.0, None, ALU.max).then_inc(s_ms, 1)
                            eng.wait_ge(s_sum, 1)
                            eng.tensor_copy(ssum[:, :], bank[3][0:ST, 0:D]).then_inc(s_ss, 1)

                ag = sb(f"ag{tag}", [P, 2, D], F32, c)
                s_al = [sem(f"s_al{tag}{i}", c) for i in range(2)]
                s_at = sem(f"s_at{tag}", c)
                s_ad = sem(f"s_ad{tag}", c)
                with nc.Block() as block:
                    @block.sync
                    def _(eng):
                        for t in range(NT):
                            if t >= 2:
                                eng.wait_ge(s_at, t - 1)
                            eng.dma_start(ag[:, t % 2, :], aggd[t * P:(t + 1) * P, :]).then_inc(s_al[t % 2], 16)

                    @block.tensor
                    def _(eng):
                        for t in range(NT):
                            eng.wait_ge(s_al[t % 2], 16 * (t // 2 + 1))
                            if t >= 2:
                                eng.wait_ge(s_ad, t - 1)
                            for k in range(2):
                                last = eng.transpose(bank[t % 2][:, k * P:k * P + P], ag[:, t % 2, k * P:k * P + P], ident[:, :])
                            last.then_inc(s_at, 1)

                    @block.vector
                    def _(eng):
                        for t in range(NT):
                            eng.wait_ge(s_at, t + 1)
                            to = aggT[:, :, t * P:(t + 1) * P]
                            eng.tensor_tensor(to, bank[t % 2][:, 0:2 * P].rearrange("p (k n) -> p k n", k=2), to,
                                              ALU.add).then_inc(s_ad, 1)

        def node_update():
            with ExitStack() as c:
                G = len(NODE_GROUPS)
                x_sb = sb("u_x", [P, NT, D], F32, c)
                ah = sb("u_ah", [P, 2, 2, 512], F32R, c)
                al = sb("u_al", [P, 2, 2, 512], F32R, c)
                g1 = sb("u_g1", [P, 4, 4, D], F32, c)
                rt = sb("u_rt", [P, 2, 2, 512], F32, c)
                rh = sb("u_rh", [P, 3, 2, 512], F32R, c)
                rl = sb("u_rl", [P, 3, 2, 512], F32R, c)
                u_z = sem("u_z", c)
                u_x = [sem(f"u_x{g}", c) for g in range(G)]
                u_xb = sem("u_xb", c)
                u_ah = sem("u_ah", c)
                u_al = sem("u_al", c)
                u_g1 = sem("u_g1", c)
                u_cp = sem("u_cp", c)
                u_st = sem("u_st", c)
                u_ag = sem("u_ag", c)
                u_ep = sem("u_ep", c)
                u_sq = sem("u_sq", c)
                u_rs = sem("u_rs", c)
                u_n = sem("u_n", c)
                u_t = sem("u_t", c)
                u_rt = sem("u_rt", c)
                u_rh = sem("u_rh", c)
                u_rl = sem("u_rl", c)
                u_g2 = sem("u_g2", c)
                u_y = sem("u_y", c)
                u_o = sem("u_o", c)
                block = c.enter_context(nc.Block())

                def pairs(g):
                    n = NODE_GROUPS[g][1]
                    return [(2 * g + q, 2 * q, min(2, n - 2 * q)) for q in range((n + 1) // 2)]

                def npairs(g):
                    return sum(len(pairs(i)) for i in range(g))

                @block.sync
                def _(eng):
                    for g, (t, n) in enumerate(NODE_GROUPS[:-1]):
                        eng.dma_start(x_sb[:, t:t + n, :],
                                      x[t * P:(t + n) * P, :].rearrange("(t p) d -> p t d", p=P)).then_inc(u_x[g], 16)
                    eng.wait_ge(u_z, 1)
                    eng.dma_start(x_sb[0:LAST, NT - 1, :], x[(NT - 1) * P:N, :]).then_inc(u_x[-1], 16)
                    for g, (t, n) in enumerate(NODE_GROUPS):
                        eng.wait_ge(u_y, npairs(g + 1))
                        if g < G - 1:
                            eng.dma_start(out[t * P:(t + n) * P, :].rearrange("(t p) d -> p t d", p=P),
                                          x_sb[:, t:t + n, :]).then_inc(u_o, 16)
                        else:
                            eng.dma_start(out[t * P:N, :], x_sb[0:LAST, t, :]).then_inc(u_o, 16)
                    eng.wait_ge(u_o, 16 * G)

                @block.gpsimd
                def _(eng):
                    for g, (t, n) in enumerate(NODE_GROUPS):
                        if g >= 2:
                            eng.wait_ge(u_ah, g + 1)
                            eng.wait_ge(u_g1, npairs(g - 1))
                            eng.wait_ge(u_al, g)
                            eng.tensor_tensor(al[:, g % 2, :, 0:n * P], aggT[:, :, t * P:(t + n) * P],
                                              ah[:, g % 2, :, 0:n * P].bitcast(F32), ALU.subtract).then_inc(u_al, 1)
                        eng.wait_ge(u_x[g], 16)
                        eng.tensor_tensor(x_sb[:, t:t + n, :], x_sb[:, t:t + n, :],
                                          bg2[:, :].rearrange("p (a d) -> p a d", a=1).broadcast_to([P, n, D]),
                                          ALU.add).then_inc(u_xb, 1)

                @block.scalar
                def _(eng):
                    def split(g):
                        t, n = NODE_GROUPS[g]
                        if g >= 2:
                            eng.wait_ge(u_g1, npairs(g - 1))
                        eng.copy(ah[:, g % 2, :, 0:n * P], aggT[:, :, t * P:(t + n) * P]).then_inc(u_ah, 1)

                    def stash(g):
                        if g >= 4:
                            eng.wait_ge(u_t, g - 3)
                        for i, (p, j, m) in enumerate(pairs(g)):
                            eng.wait_ge(u_g1, npairs(g) + i + 1)
                            eng.copy(g1[:, g % 4, j:j + m, :],
                                     bank[p % 4][:, 0:m * D].rearrange("p (j d) -> p j d", j=m)).then_inc(u_cp, 1)

                    def root(g):
                        t, n = NODE_GROUPS[g]
                        eng.wait_ge(u_ep, g + 1)
                        eng.activation(rs[:, t:t + n], rs[:, t:t + n], ACT.Sqrt).then_inc(u_sq, 1)

                    def lift(g):
                        t, n = NODE_GROUPS[g]
                        eng.wait_ge(u_t, g + 1)
                        if g >= 2:
                            eng.wait_ge(u_rl, g - 1)
                        if g >= 3:
                            eng.wait_ge(u_g2, npairs(g - 2))
                        for k in range(2):
                            last = eng.activation(rt[:, g % 2, k, 0:n * P], bank[4 + k][:, 0:n * P], ACT.Relu,
                                                  bias=lnb[:, k:k + 1], scale=lng[:, k:k + 1])
                        last.then_inc(u_rt, 1)
                        eng.wait_ge(u_rt, g + 1)
                        eng.copy(rh[:, g % 3, :, 0:n * P], rt[:, g % 2, :, 0:n * P]).then_inc(u_rh, 1)

                    split(0)
                    split(1)
                    for s in range(G + 3):
                        if 0 <= s - 2 < G:
                            root(s - 2)
                        if s < G:
                            stash(s)
                        if 0 <= s - 3 < G:
                            lift(s - 3)
                        if s + 2 < G:
                            split(s + 2)

                @block.vector
                def _(eng):
                    eng.memset(x_sb[96:P, NT - 1, :], 0.0).then_inc(u_z, 1)
                    for g, (t, n) in enumerate(NODE_GROUPS[:2]):
                        eng.wait_ge(u_ah, g + 1)
                        eng.tensor_tensor(al[:, g, :, :], aggT[:, :, t * P:(t + n) * P],
                                          ah[:, g, :, :].bitcast(F32), ALU.subtract).then_inc(u_al, 1)

                    def stats(g):
                        t, n = NODE_GROUPS[g]
                        for i, (p, j, m) in enumerate(pairs(g)):
                            eng.wait_ge(u_cp, npairs(g) + i + 1)
                            for k in range(j, j + m):
                                last = eng.bn_stats(st[:, t + k, :], g1[:, g % 4, k, :])
                        last.then_inc(u_st, 1)

                    def moments(g):
                        t, n = NODE_GROUPS[g]
                        eng.wait_ge(u_st, g + 1)
                        for k in range(t, t + n):
                            last = eng.bn_aggr(mv[:, k, :], st[:, k, :])
                        last.then_inc(u_ag, 1)
                        eng.wait_ge(u_ag, g + 1)
                        eng.tensor_scalar(rs[:, t:t + n], mv[:, t:t + n, 1], EPS, None, ALU.add).then_inc(u_ep, 1)

                    def norm(g):
                        t, n = NODE_GROUPS[g]
                        eng.wait_ge(u_sq, g + 1)
                        eng.reciprocal(rs[:, t:t + n], rs[:, t:t + n]).then_inc(u_rs, 1)
                        eng.wait_ge(u_rs, g + 1)
                        for j in range(n):
                            last = eng.tensor_scalar(g1[:, g % 4, j, :], g1[:, g % 4, j, :], mv[:, t + j, 0:1],
                                                     rs[:, t + j:t + j + 1], ALU.subtract, ALU.mult)
                        last.then_inc(u_n, 1)

                    def low(g):
                        n = NODE_GROUPS[g][1]
                        eng.wait_ge(u_rh, g + 1)
                        eng.tensor_tensor(rl[:, g % 3, :, 0:n * P], rt[:, g % 2, :, 0:n * P],
                                          rh[:, g % 3, :, 0:n * P].bitcast(F32), ALU.subtract).then_inc(u_rl, 1)

                    def finish(g):
                        t, n = NODE_GROUPS[g]
                        eng.wait_ge(u_xb, g + 1)
                        for i, (p, j, m) in enumerate(pairs(g)):
                            eng.wait_ge(u_g2, npairs(g) + i + 1)
                            eng.tensor_tensor(x_sb[:, t + j:t + j + m, :],
                                              bank[6 + p % 2][:, 0:m * D].rearrange("p (j d) -> p j d", j=m),
                                              x_sb[:, t + j:t + j + m, :], ALU.add).then_inc(u_y, 1)

                    for s in range(G + 6):
                        if 0 <= s - 6 < G:
                            finish(s - 6)
                        if 0 <= s - 4 < G:
                            low(s - 4)
                        if 0 <= s - 2 < G:
                            norm(s - 2)
                        if 0 <= s - 1 < G:
                            stats(s - 1)
                            moments(s - 1)

                @block.tensor
                def _(eng):
                    def product(o, high, low, w, e0, start):
                        for k in range(2):
                            eng.matmul(o, high[:, k, e0:e0 + P], wgr[:, w, k, :], start=(start and k == 0), stop=False)
                            eng.matmul(o, high[:, k, e0:e0 + P], wgr[:, w + 1, k, :], start=False, stop=False)
                            last = eng.matmul(o, low[:, k, e0:e0 + P], wgr[:, w, k, :], start=False, stop=(k == 1))
                        return last

                    def up(g):
                        eng.wait_ge(u_al, g + 1)
                        for i, (p, j, m) in enumerate(pairs(g)):
                            if g >= 2:
                                eng.wait_ge(u_cp, npairs(g - 2) + i + 1)
                            for q in range(m):
                                o = bank[p % 4][:, q * D:q * D + D]
                                eng.matmul(o, onr[:, :], g1r[:, :], start=True, stop=False)
                                last = product(o, ah[:, g % 2, :, :], al[:, g % 2, :, :], 0, (j + q) * P, False)
                            last.then_inc(u_g1, 1)

                    def turn(g):
                        n = NODE_GROUPS[g][1]
                        eng.wait_ge(u_n, g + 1)
                        if g >= 1:
                            eng.wait_ge(u_rt, g)
                        for j in range(n):
                            for k in range(2):
                                last = eng.transpose(bank[4 + k][:, j * P:j * P + P],
                                                     g1[:, g % 4, j, k * P:k * P + P], ident[:, :])
                        last.then_inc(u_t, 1)

                    def down(g):
                        eng.wait_ge(u_rl, g + 1)
                        for i, (p, j, m) in enumerate(pairs(g)):
                            if g >= 1:
                                eng.wait_ge(u_y, npairs(g - 1) + i + 1)
                            for q in range(m):
                                last = product(bank[6 + p % 2][:, q * D:q * D + D], rh[:, g % 3, :, :],
                                               rl[:, g % 3, :, :], 2, (j + q) * P, True)
                            last.then_inc(u_g2, 1)

                    for s in range(G + 5):
                        if s < G:
                            up(s)
                        if 0 <= s - 3 < G:
                            turn(s - 3)
                        if 0 <= s - 5 < G:
                            down(s - 5)

        with early:
            prepare()
            edge_path()
        crowded = nc.values_load(flag_i[0:1, 0:1], min_val=0, max_val=P)
        with nc.If(crowded > 0):
            nodes_again()
            general_path("b")
        node_update()


def kernel(**inputs):
    import numpy as _np
    import concourse.bacc as _bacc
    from concourse import mybir as _mybir
    from concourse.bass_utils import run_bass_kernel_spmd as _run

    w = {k: _np.asarray(v) for k, v in inputs.items()}
    p = "L0_gnn_"
    data = [
        ("x", w["x"]), ("src", w["src"]), ("dst", w["dst"]),
        ("src_m", w["src"][:FULL * P].reshape(FULL, P).T), ("dst_m", w["dst"][:FULL * P].reshape(FULL, P).T),
        ("pol_m", w["edge_attr_65"][:FULL * P, 0].reshape(FULL, P).T), ("pol", w["edge_attr_65"][:, 0]),
        ("first", w["dst"][::GE]),
        ("attrT", _np.ascontiguousarray(w["edge_attr_65"].T)),
        ("W_e1T", _np.ascontiguousarray(w[p + "W_e1"].T)), ("b_e1", w[p + "b_e1"].reshape(2, P).T), ("b_e1r", w[p + "b_e1"]),
        ("W_e2", w[p + "W_e2"]), ("b_e2", w[p + "b_e2"].reshape(2, P).T),
        ("W_leT", _np.ascontiguousarray(w[p + "W_le"].T)), ("b_le", w[p + "b_le"]),
        ("W_g1T", _np.ascontiguousarray(w[p + "W_g1"].T)), ("b_g1", w[p + "b_g1"]),
        ("ln_g", w[p + "ln_g"].reshape(2, P).T), ("ln_b", w[p + "ln_b"].reshape(2, P).T),
        ("W_g2T", _np.ascontiguousarray(w[p + "W_g2"].T)), ("b_g2", w[p + "b_g2"]),
    ]
    nc = _bacc.Bacc("TRN2", target_bir_lowering=False, num_devices=1)
    arrays, args = {}, []
    for name, a in data:
        a = _np.ascontiguousarray(a)
        arrays[f"in_{name}"] = a
        args.append(nc.dram_tensor(f"in_{name}", a.shape, _mybir.dt.from_np(a.dtype), kind="ExternalInput").ap())
    o = nc.dram_tensor("out_0", (N, D), _mybir.dt.float32, kind="ExternalOutput").ap()
    gnn(nc, *args, o)
    r = _run(nc, [arrays], core_ids=[0])
    return r.results[0]["out_0"]
```
